# Optimizing a Trainium2 kernel written in Bass

```python
import numpy as np
import jax
import jax.numpy as jnp

def _softmax(x, axis=-1):
    return jax.nn.softmax(x, axis=axis)

def _gelu(x):
    return jax.nn.gelu(x, approximate=True)

def _silu(x):
    return jax.nn.silu(x)

def _sigmoid(x):
    return jax.nn.sigmoid(x)

def _layernorm(x, axis=-1, eps=1e-05):
    m = jnp.mean(x, axis=axis, keepdims=True)
    v = jnp.var(x, axis=axis, keepdims=True)
    return (x - m) / jnp.sqrt(v + eps)

def _scatter_add(tgt, idx, src, axis=0):
    return tgt.at[idx].add(src)

def _segment_sum(src, seg, n):
    return jax.ops.segment_sum(src, seg, n)
kernel_name = 'mk_flamingo_gated_d1_seqx_r8_f5fe1d'

def setup_inputs(seed: int=0):
    np.random.seed(seed)
    _w = jnp.asarray

    def _rec_inputs():
        import jax
        import jax.numpy as jnp
        _rk = jax.random.key(seed)
        x = 7.22e-05 + 1 * jax.random.normal(jax.random.fold_in(_rk, 1), (64, 64, 256), jnp.float32)
        _lenS = 64 - jax.random.randint(jax.random.fold_in(_rk, 7), (64,), 0, max(1, 64 // 4) + 1, jnp.int32)
        _lenS2 = 64 - jax.random.randint(jax.random.fold_in(_rk, 8), (64,), 0, max(1, 64 // 4) + 1, jnp.int32)
        _ctx_2048P = jax.random.normal(jax.random.fold_in(_rk, 11), (64, 16, 256), jnp.float32)
        _ctx_2048c = jax.random.dirichlet(jax.random.fold_in(_rk, 511), 0.3 * jnp.ones((16,), jnp.float32), (64, 64))
        _ctx_2048t = jnp.einsum('bsk,bkd->bsd', _ctx_2048c, _ctx_2048P)
        _ctx_2048t = _ctx_2048t * jax.lax.rsqrt(jnp.mean(jnp.square(_ctx_2048t)) + 1e-12) * 0.953939
        ctx_2048 = 4.13588e-05 + 0.999923 * (_ctx_2048t + 0.3 * jax.random.normal(jax.random.fold_in(_rk, 611), (64, 64, 256), jnp.float32))
        _g = jax.random.normal(jax.random.fold_in(_rk, 9001), (2, 1), jnp.float32)
        _g = jnp.sign(_g) * jnp.maximum(jnp.abs(_g), 1.0) + (_g == 0) * 1.0
        g_xattn = _g[0]
        g_ffn = _g[1]
        return (x, ctx_2048, g_xattn, g_ffn)
    x, ctx_2048, g_xattn, g_ffn = _rec_inputs()

    def _L0_xattn_setup():
        import math
        import jax, jax.numpy as jnp
        import numpy as np
        HEADS = 16
        MASKED_BIAS = -10000.0

        def _mha(q, k, v):
            B, Sq, D = q.shape
            Sk = k.shape[-2]
            hd = D // HEADS
            qh = q.reshape(B, Sq, HEADS, hd).transpose(0, 2, 1, 3)
            kh = k.reshape(B, Sk, HEADS, hd).transpose(0, 2, 1, 3)
            vh = v.reshape(B, Sk, HEADS, hd).transpose(0, 2, 1, 3)
            scores = jnp.einsum('bhqd,bhkd->bhqk', qh, kh) / math.sqrt(hd)
            qi = jnp.arange(Sq)[:, None] + (Sk - Sq)
            ki = jnp.arange(Sk)[None, :]
            causal = ki <= qi
            scores = jnp.where(causal[None, None], scores, jnp.asarray(MASKED_BIAS, scores.dtype))
            attn = jax.nn.softmax(scores, axis=-1)
            out = jnp.einsum('bhqk,bhkd->bhqd', attn, vh)
            return out.transpose(0, 2, 1, 3).reshape(B, Sq, D)
        key = jax.random.key(seed)
        kq, kk, kv = jax.random.split(key, 3)
        B, S, D = (4, 128, 256)
        q = jax.random.normal(kq, (B, S, D), dtype=jnp.float32)
        k = jax.random.normal(kk, (B, S, D), dtype=jnp.float32)
        v = jax.random.normal(kv, (B, S, D), dtype=jnp.float32)
        return {'q': q, 'k': k, 'v': v}
    _L0_xattn_all = _L0_xattn_setup()
    _L0_xattn_in = {k: v for k, v in _L0_xattn_all.items() if k in ()}
    del _L0_xattn_all

    def _L0_ffn_setup():
        import jax, jax.numpy as jnp
        import numpy as np
        HIDDEN = 256
        INTER = 96
        N_EXPERTS = 32
        TOP_K = 8
        key = jax.random.key(seed)
        k = jax.random.split(key, 5)
        s = 1.0 / np.sqrt(HIDDEN)
        return {'hidden_states': jax.random.normal(k[0], (1, 128, HIDDEN), jnp.float32), 'gate_w': jax.random.normal(k[1], (HIDDEN, N_EXPERTS), jnp.float32) * s, 'w_gate': jax.random.normal(k[2], (N_EXPERTS, HIDDEN, INTER), jnp.float32) * s, 'w_up': jax.random.normal(k[3], (N_EXPERTS, HIDDEN, INTER), jnp.float32) * s, 'w_down': jax.random.normal(k[4], (N_EXPERTS, INTER, HIDDEN), jnp.float32) * (1.0 / np.sqrt(INTER))}
    _L0_ffn_all = _L0_ffn_setup()
    _L0_ffn_in = {k: v for k, v in _L0_ffn_all.items() if k in ('gate_w', 'w_gate', 'w_up', 'w_down')}
    del _L0_ffn_all
    return {'x': x, 'ctx_2048': ctx_2048, 'g_xattn': g_xattn, 'g_ffn': g_ffn, 'L0_ffn_gate_w': _L0_ffn_in['gate_w'], 'L0_ffn_w_gate': _L0_ffn_in['w_gate'], 'L0_ffn_w_up': _L0_ffn_in['w_up'], 'L0_ffn_w_down': _L0_ffn_in['w_down']}

def reference(x, ctx_2048, g_xattn, g_ffn, L0_ffn_gate_w, L0_ffn_w_gate, L0_ffn_w_up, L0_ffn_w_down):
    import jax
    import jax.numpy as jnp

    def _L0_xattn_ref(q, k, v):
        import math
        import jax, jax.numpy as jnp
        import numpy as np
        HEADS = 16
        MASKED_BIAS = -10000.0

        def _mha(q, k, v):
            B, Sq, D = q.shape
            Sk = k.shape[-2]
            hd = D // HEADS
            qh = q.reshape(B, Sq, HEADS, hd).transpose(0, 2, 1, 3)
            kh = k.reshape(B, Sk, HEADS, hd).transpose(0, 2, 1, 3)
            vh = v.reshape(B, Sk, HEADS, hd).transpose(0, 2, 1, 3)
            scores = jnp.einsum('bhqd,bhkd->bhqk', qh, kh) / math.sqrt(hd)
            qi = jnp.arange(Sq)[:, None] + (Sk - Sq)
            ki = jnp.arange(Sk)[None, :]
            causal = ki <= qi
            scores = jnp.where(causal[None, None], scores, jnp.asarray(MASKED_BIAS, scores.dtype))
            attn = jax.nn.softmax(scores, axis=-1)
            out = jnp.einsum('bhqk,bhkd->bhqd', attn, vh)
            return out.transpose(0, 2, 1, 3).reshape(B, Sq, D)
        return _mha(q, k, v)

    def _L0_ffn_ref(hidden_states, gate_w, w_gate, w_up, w_down):
        import jax, jax.numpy as jnp
        import numpy as np
        HIDDEN = 256
        INTER = 96
        N_EXPERTS = 32
        TOP_K = 8
        B, S, H = hidden_states.shape
        E = gate_w.shape[1]
        x = hidden_states.reshape(-1, H)
        T = x.shape[0]
        K = TOP_K
        P = T * K
        C = 2 * (P // E)
        probs = jax.nn.softmax(x @ gate_w, axis=-1)
        w, sel = jax.lax.top_k(probs, K)
        w = w / jnp.sum(w, axis=-1, keepdims=True)
        flat_e = sel.reshape(-1)
        flat_t = jnp.repeat(jnp.arange(T), K)
        flat_w = w.reshape(-1)
        order = jnp.argsort(flat_e)
        se = flat_e[order]
        start = jnp.searchsorted(se, jnp.arange(E))
        pos = jnp.arange(P) - start[se]
        slot = jnp.where(pos < C, se * C + pos, E * C)
        slot_pair = jnp.full((E * C,), P, dtype=jnp.int32).at[slot].set(order.astype(jnp.int32), mode='drop')
        t_slot = jnp.concatenate([flat_t, jnp.array([T])])[slot_pair]
        w_slot = jnp.concatenate([flat_w, jnp.zeros((1,), flat_w.dtype)])[slot_pair]
        x_pad = jnp.concatenate([x, jnp.zeros((1, H), x.dtype)], axis=0)
        xg = x_pad[t_slot].reshape(E, C, H)
        g = jnp.einsum('ech,ehi->eci', xg, w_gate)
        u = jnp.einsum('ech,ehi->eci', xg, w_up)
        y = jnp.einsum('eci,eih->ech', jax.nn.silu(g) * u, w_down).reshape(E * C, H)
        out = jnp.zeros((T + 1, H), x.dtype).at[t_slot].add(w_slot[:, None] * y)
        return out[:T].reshape(B, S, H)
    x = x + jnp.tanh(g_xattn[0]) * _L0_xattn_ref(_layernorm(x, axis=-1), ctx_2048, ctx_2048)
    x = x + jnp.tanh(g_ffn[0]) * _L0_ffn_ref(_layernorm(x, axis=-1), L0_ffn_gate_w, L0_ffn_w_gate, L0_ffn_w_up, L0_ffn_w_down)
    return x

_drawn_inputs = setup_inputs


def setup_inputs(seed=0):
    import zlib

    import numpy as np

    out = dict(_drawn_inputs(seed))
    spreads = {}
    factors = {}
    for name, (base, spread) in spreads.items():
        noise = np.random.default_rng([zlib.crc32(name.encode()), seed]).standard_normal(out[name].shape)
        drawn = base * np.exp(spread * noise) if base else spread * noise
        out[name] = jnp.asarray(drawn.astype(out[name].dtype))
    for name, factor in factors.items():
        out[name] = (out[name] * factor).astype(out[name].dtype)
    return out
```

```python
from contextlib import ExitStack

import concourse.bass as bass
from concourse import mybir

P = 128
F32 = mybir.dt.float32
F16 = mybir.dt.float16
BF16 = mybir.dt.bfloat16
I32 = mybir.dt.int32
ALU = mybir.AluOpType
ACT = mybir.ActivationFunctionType
AX = mybir.AxisListType
RMAX = bass.bass_isa.ReduceOp.max

HEADS = 16
TOP_K = 8
EPS = 1e-5
MASKED = -10000.0
EXP_FLOOR = -104.0


def build(nc, x, ctx_in, g_xattn, g_ffn, gate_w, w_gate, w_up, w_down, out):
    B, S, D = x.shape
    E, _, INTER = w_gate.shape
    T = B * S
    NT = T // P
    HD = D // HEADS
    KT = D // P
    CAP = 2 * (T * TOP_K // E)
    G4 = P // 32
    NM = E // G4
    NI = INTER // 32
    NB = 512
    TPB = NB // P
    SLOT = NI * P * KT
    assert S == 64 and HD == 16 and KT == 2 and SLOT == NI * D

    x_rows = x.rearrange("b s d -> (b s) d")
    ctx_rows = ctx_in.rearrange("b s d -> (b s) d")
    out_rows = out.rearrange("b s d -> (b s) d")

    persist = ExitStack()

    def sbuf(stack, name, shape, dt):
        return stack.enter_context(nc.sbuf_tensor(name, shape, dt))

    def psum(stack, name, shape, dt):
        return stack.enter_context(nc.psum_tensor(name, shape, dt))

    def sem(name):
        return persist.enter_context(nc.semaphore(name))

    with persist:
        xs = sbuf(persist, "xs", [P, NT, D], F32)
        wall = sbuf(persist, "wall", [P, (3 * NM + 1) * SLOT * 2], F16)
        wall32 = wall[:, :].bitcast(F32)
        gatew = sbuf(persist, "gatew", [P, KT, E], F32)
        identf = sbuf(persist, "identf", [P, P], F32)
        identb = sbuf(persist, "identb", [P, P], BF16)
        tri = sbuf(persist, "tri", [P, P], BF16)
        onesb = sbuf(persist, "onesb", [P, P], BF16)
        sel = sbuf(persist, "sel", [3 * E, NM, P], BF16)
        parity = sbuf(persist, "parity", [P, 2], F32)
        gates = sbuf(persist, "gates", [P, 2], F32)
        tanhg = sbuf(persist, "tanhg", [P, 2], F32)
        stats = sbuf(persist, "stats", [P, NT, 6], F32)
        mean = sbuf(persist, "mean", [P, NT], F32)
        rstd = sbuf(persist, "rstd", [P, NT], F32)
        va = sbuf(persist, "va", [P, NT], F32)
        vb = sbuf(persist, "vb", [P, NT], F32)
        wmax = sbuf(persist, "wmax", [P, 3], F32)
        wmax_all = sbuf(persist, "wmax_all", [P, 3], F32)
        pow2 = sbuf(persist, "pow2", [P, 3], F32)
        inv2 = sbuf(persist, "inv2", [P, 3], F32)
        inv24 = sbuf(persist, "inv24", [P, 3 * NM], F32)
        wfac = sbuf(persist, "wfac", [P, 1], F32)
        yfac = sbuf(persist, "yfac", [P, 1], F32)

        x_in = [sem(f"x_in{i}") for i in range(4)]
        small_in = sem("small_in")
        w_in = [sem(f"w_in{i}") for i in range(3)]
        zeros_set, masks_set = sem("zeros_set"), sem("masks_set")
        tanh_done = sem("tanh_done")
        stat_step = sem("stat_step")
        sqrt_done = sem("sqrt_done")
        wmax_done, wmax_shared, scale_step = sem("wmax_done"), sem("wmax_shared"), sem("scale_step")
        split_done = sem("split_done")

        def finish_stats(dve, base):
            me, m2e, mo, m2o = (stats[:, :, k] for k in (1, 2, 4, 5))
            count = [base]

            def step(instruction):
                count[0] += 1
                instruction.then_inc(stat_step, 1)
                dve.wait_ge(stat_step, count[0])

            step(nc.vector.tensor_tensor(va[:, :], me, mo, ALU.subtract))
            step(nc.vector.tensor_tensor(mean[:, :], me, mo, ALU.add))
            step(nc.vector.tensor_tensor(vb[:, :], m2e, m2o, ALU.add))
            step(nc.vector.tensor_scalar(mean[:, :], mean[:, :], 0.5, None, ALU.mult))
            step(nc.vector.scalar_tensor_tensor(va[:, :], va[:, :], 0.25, va[:, :], ALU.mult, ALU.mult))
            step(nc.vector.tensor_scalar(vb[:, :], vb[:, :], 1.0 / D, EPS, ALU.mult, ALU.add))
            step(nc.vector.tensor_tensor(vb[:, :], vb[:, :], va[:, :], ALU.add))
            return count[0]

        def finish_rstd(dve, base, which):
            count = [base]

            def step(instruction):
                count[0] += 1
                instruction.then_inc(stat_step, 1)
                dve.wait_ge(stat_step, count[0])

            dve.wait_ge(sqrt_done, which)
            step(nc.vector.reciprocal(rstd[:, :], va[:, :]))
            step(nc.vector.tensor_tensor(va[:, :], rstd[:, :], rstd[:, :], ALU.mult))
            step(nc.vector.tensor_tensor(va[:, :], va[:, :], vb[:, :], ALU.mult))
            step(nc.vector.tensor_scalar(va[:, :], va[:, :], -0.5, 1.5, ALU.mult, ALU.add))
            step(nc.vector.tensor_tensor(rstd[:, :], rstd[:, :], va[:, :], ALU.mult))
            return count[0]

        STATS = 7
        RSTD = 5

        with nc.Block() as block:
            @block.sync
            def _(sp):
                for i in range(4):
                    n = NT // 4
                    sp.dma_start(xs[:, i * n:(i + 1) * n, :],
                                 x_rows[i * n * P:(i + 1) * n * P, :].rearrange("(t p) d -> p t d", p=P)
                                 ).then_inc(x_in[i], 16)
                sp.dma_start(gatew[:, :, :], gate_w.rearrange("(k p) e -> p k e", p=P)).then_inc(small_in, 16)
                for i, g in enumerate((g_xattn, g_ffn)):
                    sp.dma_start(gates[:, i:i + 1], g.rearrange("(a b) -> a b", b=1).to_broadcast([P, 1])
                                 ).then_inc(small_in, 16)
                for n, w in ((0, w_gate), (1, w_up)):
                    at = (1 + n * NM) * SLOT
                    sp.dma_start(wall32[:, at:at + NM * SLOT].rearrange("p (a i) -> p a i", i=INTER),
                                 w.rearrange("e (k p) i -> p (e k) i", p=P)).then_inc(w_in[n], 16)
                at = (1 + 2 * NM) * SLOT
                for q in range(G4):
                    for i in range(NI):
                        sp.dma_start(wall32[32 * q:32 * q + 32, at:at + NM * SLOT].rearrange(
                            "p (m i n) -> p i m n", m=NM, i=NI)[:, i],
                            w_down.rearrange("(m q) (i r) n -> q i r m n", q=G4, r=32)[q, i]).then_inc(w_in[2], 16)

            @block.gpsimd
            def _(pool):
                nc.gpsimd.memset(identf[:, :], 0.0).then_inc(zeros_set, 1)
                nc.gpsimd.memset(identb[:, :], 0.0).then_inc(zeros_set, 1)
                nc.gpsimd.memset(tri[:, :], 1.0).then_inc(zeros_set, 1)
                nc.gpsimd.memset(sel[:, :, :], 0.0).then_inc(zeros_set, 1)
                nc.gpsimd.memset(parity[:, :], 1.0).then_inc(zeros_set, 1)
                nc.gpsimd.memset(onesb[:, :], 1.0).then_inc(zeros_set, 1)
                pool.wait_ge(zeros_set, 6)
                made = [0]

                def mask(v, compare, fill, base, pattern, per_row):
                    nc.gpsimd.affine_select(out=v, in_=v, compare_op=compare, fill=fill, base=base, pattern=pattern,
                                            channel_multiplier=per_row).then_inc(masks_set, 1)
                    made[0] += 1
                    pool.wait_ge(masks_set, made[0])

                for m in (identf, identb):
                    mask(m[:, :], ALU.not_equal, 1.0, 0, [[-1, P]], 1)
                mask(tri[:, :], ALU.is_gt, 0.0, 0, [[1, P]], -1)
                for part in range(3):
                    mask(sel[part * E:(part + 1) * E, :, :].rearrange("p m (q r) -> p m q r", q=G4),
                         ALU.not_equal, 1.0, 0, [[-G4, NM], [-1, G4], [0, 32]], 1)
                for g in range(G4):
                    even, odd = (parity[32 * g:32 * g + 32, h:h + 1] for h in range(2))
                    mask(even, ALU.is_ge, 0.0, HD - 1, [[0, 1]], -1)
                    mask(odd, ALU.is_ge, 0.0, -HD, [[0, 1]], 1)

            @block.vector
            def _(dve):
                for i in range(4):
                    dve.wait_ge(x_in[i], 16)
                    with nc.vector.Fori(i * NT // 4, (i + 1) * NT // 4) as t:
                        nc.vector.bn_stats(stats[:, bass.ds(t, 1), :], xs[:, bass.ds(t, 1), :]).then_inc(stat_step, 1)
                dve.wait_ge(stat_step, NT)
                finish_stats(dve, NT)
                finish_rstd(dve, NT + STATS, 1)

            @block.scalar
            def _(act):
                act.wait_ge(stat_step, NT + STATS)
                nc.scalar.activation(va[:, :], vb[:, :], ACT.Sqrt).then_inc(sqrt_done, 1)
                act.wait_ge(small_in, 48)
                nc.scalar.activation(tanhg[:, :], gates[:, :], ACT.Tanh).then_inc(tanh_done, 1)
                act.wait_ge(tanh_done, 1)

        with ExitStack() as phase:
            cnat = [sbuf(phase, f"cnat{i}", [P, D], F32) for i in range(2)]
            cdup = [sbuf(phase, f"cdup{i}", [P, 2, D], F32) for i in range(2)]
            xn = [sbuf(phase, f"xn{i}", [P, D], F32) for i in range(2)]
            qT = [sbuf(phase, f"qT{i}", [P, KT, P], F32) for i in range(2)]
            kpair = [sbuf(phase, f"kpair{i}", [P, KT * 2, 2, S], F32) for i in range(2)]
            sc = [sbuf(phase, f"sc{i}", [P, HEADS, S], F32) for i in range(2)]
            pr = [sbuf(phase, f"pr{i}", [P, HEADS * S], F32) for i in range(2)]
            pT = [sbuf(phase, f"pT{i}", [P, HEADS // 2, P], F32) for i in range(2)]
            vpair = [sbuf(phase, f"vpair{i}", [P, 2, HEADS // 2, 2, HD + 1], F32) for i in range(2)]
            smax = sbuf(phase, "smax", [P, HEADS], F32)
            rden = sbuf(phase, "rden", [P, HEADS], F32)
            att = sbuf(phase, "att", [P, HEADS, HD], F32)
            qk_ps = psum(phase, "qk_ps", [P, 2 * KT, P], F32)
            s_ps = psum(phase, "s_ps", [P, G4, 512], F32)
            pT_ps = psum(phase, "pT_ps", [P, HEADS // 2, P], F32)
            o_ps = psum(phase, "o_ps", [P, 512], F32)
            o_v = o_ps[:, 0:HEADS * (HD + 1)].rearrange("p (h d) -> p h d", d=HD + 1)

            cnat_in = [sem(f"cnat_in{i}") for i in range(2)]
            cdup_in = [sem(f"cdup_in{i}") for i in range(2)]
            ln_done, tqk_done, q_done, k_done = sem("ln_done"), sem("tqk_done"), sem("q_done"), sem("k_done")
            s_done, s_copied, masked, max_done, sub_done = (sem(n) for n in (
                "s_done", "s_copied", "masked", "max_done", "sub_done"))
            exp_done, tp_done, pT_done, v_done, pv_done = (sem(n) for n in (
                "exp_done", "tp_done", "pT_done", "v_done", "pv_done"))
            rden_step, att_done, x1_done, v_init = sem("rden_step"), sem("att_done"), sem("x1_done"), sem("v_init")
            mask_turn = sem("mask_turn")

            FIRST, LAST = -3, NT + 3
            LOOP = (4, NT - 4)

            def pipeline(engine, step, first=FIRST, last=LAST, loop=LOOP):
                for n in range(first, loop[0]):
                    step(n, n)
                with engine.Fori(loop[0], loop[1] - 1, 2) as n:
                    step(n, 0)
                    step(n + 1, 1)
                for n in range(loop[1], last):
                    step(n, n)

            def has(j):
                return not isinstance(j, int) or 0 <= j < NT

            def wait(engine, s, count):
                if not isinstance(count, int) or count > 0:
                    engine.wait_ge(s, count)

            def landed(j, b, per):
                return (j - b) * 8 * per + 16 * per

            with nc.Block() as block:
                @block.sync
                def _(sp):
                    def step(n, k):
                        j, b = n + 3, (k + 3) % 2
                        if has(j):
                            wait(sp, tqk_done, j - 1)
                            sp.dma_start(cnat[b][:, :], ctx_rows[bass.ds(j * P, P), :]).then_inc(cnat_in[b], 16)
                        j, b = n, k % 2
                        if has(j):
                            wait(sp, v_done, j - 1)
                            src = ctx_rows[bass.ds(j * P, P), :].rearrange("(b s) d -> s b d", b=2)
                            for half in range(2):
                                sp.dma_start(cdup[b][64 * half:64 * half + 64, :, :], src).then_inc(cdup_in[b], 16)
                    pipeline(nc.sync, step)

                @block.tensor
                def _(pe):
                    def step(n, k):
                        j, b = n + 1, (k + 1) % 2
                        if has(j):
                            wait(pe, ln_done, j + 1)
                            wait(pe, cnat_in[b], landed(j, b, 1))
                            wait(pe, q_done, j)
                            wait(pe, k_done, j)
                            for c in range(KT):
                                nc.tensor.transpose(qk_ps[:, c, :], xn[b][:, c * P:(c + 1) * P], identf[:, :])
                            for c in range(KT):
                                last = nc.tensor.transpose(qk_ps[:, KT + c, :], cnat[b][:, c * P:(c + 1) * P],
                                                           identf[:, :])
                            last.then_inc(tqk_done, 1)
                        j, b = n - 2, k % 2
                        if has(j):
                            wait(pe, exp_done, j + 1)
                            wait(pe, pT_done, j)
                            for c in range(HEADS // 2):
                                last = nc.tensor.transpose(pT_ps[:, c, :], pr[b][:, c * P:(c + 1) * P], identf[:, :])
                            last.then_inc(tp_done, 1)
                        j, b = n, k % 2
                        if has(j):
                            wait(pe, q_done, j + 1)
                            wait(pe, k_done, j + 1)
                            wait(pe, s_copied, j)
                            for c in range(KT):
                                for h in range(2):
                                    for g in range(G4):
                                        rows = slice(32 * g, 32 * g + 32)
                                        last = nc.tensor.matmul(
                                            s_ps[64 * h:64 * h + 64, g, c * P:(c + 1) * P],
                                            qT[b][rows, c, 64 * h:64 * h + 64],
                                            kpair[b][rows, 2 * c + h, :, :].rearrange("p a s -> p (a s)"),
                                            start=True, stop=True)
                            last.then_inc(s_done, 1)
                        j, b = n - 3, (k + 1) % 2
                        if has(j):
                            wait(pe, pT_done, j + 1)
                            wait(pe, v_done, j + 1)
                            wait(pe, att_done, j)
                            for c in range(HEADS // 2):
                                g, half = c // 2, c % 2
                                pair = half * G4 + g
                                for h in range(2):
                                    last = nc.tensor.matmul(
                                        o_ps[64 * h:64 * h + 64, pair * 34:pair * 34 + 34],
                                        pT[b][:, c, 64 * h:64 * h + 64],
                                        vpair[b][:, h, pair, :, :].rearrange("p a d -> p (a d)"),
                                        start=True, stop=True)
                            last.then_inc(pv_done, 1)
                    pipeline(nc.tensor, step)

                @block.scalar
                def _(act):
                    def step(n, k):
                        j, b = n - 2, k % 2
                        if has(j):
                            wait(act, sub_done, j + 1)
                            wait(act, tp_done, j - 1)
                            nc.scalar.activation(pr[b][:, :], sc[b][:, :, :].rearrange("p h s -> p (h s)"),
                                                 ACT.Exp).then_inc(exp_done, 1)
                        j, b = n + 1, (k + 1) % 2
                        if has(j):
                            wait(act, k_done, j + 1)
                            wait(act, s_done, j - 1)
                            nc.scalar.activation(qT[b][:, :, :], qk_ps[:, 0:KT, :], ACT.Copy).then_inc(q_done, 1)
                        j, b = n - 2, k % 2
                        if has(j):
                            wait(act, tp_done, j + 1)
                            wait(act, pv_done, j - 1)
                            nc.scalar.activation(pT[b][:, :, :], pT_ps[:, :, :], ACT.Copy).then_inc(pT_done, 1)
                        j, b = n, k % 2
                        if has(j):
                            wait(act, s_done, j + 1)
                            wait(act, exp_done, j - 1)
                            nc.scalar.activation(sc[b][:, :, :].rearrange("p (g a) s -> p g (a s)", g=G4),
                                                 s_ps[:, :, 0:2 * P], ACT.Copy, scale=HD ** -0.5).then_inc(s_copied, 1)
                    pipeline(nc.scalar, step)
                    act.wait_ge(stat_step, NT + STATS + RSTD + NT + STATS)
                    nc.scalar.activation(va[:, :], vb[:, :], ACT.Sqrt).then_inc(sqrt_done, 1)

                @block.vector
                def _(dve):
                    for b in range(2):
                        nc.vector.memset(vpair[b][:, :, :, :, 0:HD], 0.0)
                        for half in range(2):
                            rows = slice(64 * half, 64 * half + 64)
                            nc.vector.memset(vpair[b][rows, :, :, half, HD:HD + 1], 1.0)
                            last = nc.vector.memset(vpair[b][rows, :, :, 1 - half, HD:HD + 1], 0.0)
                    last.then_inc(v_init, 1)
                    dve.wait_ge(v_init, 1)

                    def step(n, k):
                        j, b = n + 1, (k + 1) % 2
                        if has(j):
                            wait(dve, tqk_done, j + 1)
                            wait(dve, s_done, j - 1)
                            nc.vector.tensor_tensor(
                                kpair[b][:, :, :, :],
                                qk_ps[:, KT:2 * KT, :].rearrange("p c (h s) -> p (c h) s", h=2)[:, :, None, :]
                                .to_broadcast([P, 2 * KT, 2, S]),
                                parity[:, None, :, None].to_broadcast([P, 2 * KT, 2, S]),
                                ALU.mult).then_inc(k_done, 1)
                        j, b = n + 2, k % 2
                        if has(j):
                            wait(dve, tqk_done, j - 1)
                            nc.vector.tensor_scalar(xn[b][:, :], xs[:, bass.ds(j, 1), :], mean[:, bass.ds(j, 1)],
                                                    rstd[:, bass.ds(j, 1)], ALU.subtract, ALU.mult
                                                    ).then_inc(ln_done, 1)
                        j, b = n - 2, k % 2
                        if has(j):
                            wait(dve, cdup_in[b], landed(j, b, 2))
                            wait(dve, pv_done, j - 1)
                            src = cdup[b][:, :, :].rearrange("p h (c a d) -> p h c a d", a=2, d=HD)
                            for half in range(2):
                                rows = slice(64 * half, 64 * half + 64)
                                last = nc.vector.tensor_copy(vpair[b][rows, :, :, half, 0:HD], src[rows, :, :, half, :])
                            last.then_inc(v_done, 1)
                        j, b = n - 1, (k + 1) % 2
                        if has(j):
                            wait(dve, masked, 2 * j + 2)
                            wait(dve, sub_done, j)
                            nc.vector.tensor_reduce(smax[:, :], sc[b][:, :, :], AX.X, ALU.max).then_inc(max_done, 1)
                            wait(dve, max_done, j + 1)
                            nc.vector.tensor_tensor(sc[b][:, :, :], sc[b][:, :, :],
                                                    smax[:, :, None].to_broadcast([P, HEADS, S]),
                                                    ALU.subtract).then_inc(sub_done, 1)
                        j = n - 3
                        if has(j):
                            wait(dve, pv_done, j + 1)
                            wait(dve, x1_done, j)
                            nc.vector.reciprocal(rden[:, :], o_v[:, :, HD]).then_inc(rden_step, 1)
                            wait(dve, rden_step, 2 * j + 1)
                            nc.vector.tensor_scalar(rden[:, :], rden[:, :], tanhg[:, 0:1], None, ALU.mult
                                                    ).then_inc(rden_step, 1)
                            wait(dve, rden_step, 2 * j + 2)
                            nc.vector.tensor_tensor(att[:, :, :], o_v[:, :, 0:HD],
                                                    rden[:, :, None].to_broadcast([P, HEADS, HD]),
                                                    ALU.mult).then_inc(att_done, 1)
                            wait(dve, att_done, j + 1)
                            row = xs[:, bass.ds(j, 1), :]
                            nc.vector.tensor_tensor(row, row, att[:, :, :].rearrange("p h d -> p (h d)")[:, None, :],
                                                    ALU.add).then_inc(x1_done, 1)
                            wait(dve, x1_done, j + 1)
                            nc.vector.bn_stats(stats[:, bass.ds(j, 1), :], row).then_inc(stat_step, 1)

                    SPLIT = 8
                    for n in range(FIRST, LOOP[0]):
                        step(n, n)
                    with nc.vector.Fori(LOOP[0], SPLIT - 1, 2) as n:
                        step(n, 0)
                        step(n + 1, 1)
                    for i in range(3):
                        at = (1 + i * NM) * SLOT
                        dve.wait_ge(w_in[i], 16 if i < 2 else 16 * G4 * NI)
                        nc.vector.tensor_reduce(wmax[:, i:i + 1], wall32[:, at:at + NM * SLOT], AX.X, ALU.max,
                                                apply_absolute_value=True).then_inc(wmax_done, 1)
                    with nc.vector.Fori(SPLIT, SPLIT + 1, 2) as n:
                        step(n, 0)
                        step(n + 1, 1)
                    dve.wait_ge(wmax_shared, 1)
                    nc.vector.tensor_scalar(pow2[:, :].bitcast(I32), wmax_all[:, :].bitcast(I32), 0x7F800000, None,
                                            ALU.bitwise_and).then_inc(scale_step, 1)
                    dve.wait_ge(scale_step, 1)
                    nc.vector.tensor_scalar(pow2[:, :], pow2[:, :], 2.0 ** -60, None, ALU.max).then_inc(scale_step, 1)
                    dve.wait_ge(scale_step, 2)
                    nc.vector.reciprocal(inv2[:, :], pow2[:, :]).then_inc(scale_step, 1)
                    dve.wait_ge(scale_step, 3)
                    nc.vector.tensor_copy(inv24[:, :].rearrange("p (t m) -> p t m", m=NM),
                                          inv2[:, :, None].to_broadcast([P, 3, NM])).then_inc(scale_step, 1)
                    nc.vector.tensor_scalar(wfac[:, :], inv2[:, 0:1], 0.125, None, ALU.mult).then_inc(scale_step, 1)
                    nc.vector.tensor_scalar(yfac[:, :], pow2[:, 0:1], pow2[:, 1:2], pow2[:, 2:3],
                                            ALU.mult, ALU.mult).then_inc(scale_step, 1)
                    dve.wait_ge(scale_step, 6)
                    nc.vector.tensor_scalar(yfac[:, :], yfac[:, :], 8.0, tanhg[:, 1:2], ALU.mult, ALU.mult
                                            ).then_inc(scale_step, 1)
                    dve.wait_ge(scale_step, 7)
                    with nc.vector.Fori(SPLIT + 2, LOOP[1] - 1, 2) as n:
                        step(n, 0)
                        step(n + 1, 1)
                    for n in range(LOOP[1], LAST):
                        step(n, n)
                    base = NT + STATS + RSTD + NT
                    dve.wait_ge(stat_step, base)
                    finish_stats(dve, base)
                    finish_rstd(dve, base + STATS, 2)

                @block.gpsimd
                def _(pool):
                    fill = nc.gpsimd.to_reg(MASKED)

                    def mask(j, b):
                        pool.wait_ge(s_copied, j + 1)
                        pool.sem_inc(mask_turn, 1)
                        for half in range(2):
                            v = sc[b][64 * half:64 * half + 64, :, :]
                            nc.gpsimd.affine_select(out=v, in_=v, compare_op=ALU.is_ge, fill=fill, base=0,
                                                    pattern=[[0, HEADS], [-1, S]], channel_multiplier=1
                                                    ).then_inc(masked, 1)

                    def split(k, expand):
                        n = SLOT
                        src = wall32[:, bass.ds((k + 1) * n, n)]
                        nc.gpsimd.tensor_tensor(src, src, inv24[:, bass.ds(k, 1)].to_broadcast([P, n]), ALU.mult
                                                ).then_inc(split_done, 1)
                        pool.wait_ge(split_done, 3 * k + 1)
                        for part in range(2):
                            for half in range(KT if expand else 1):
                                if expand:
                                    s = src.rearrange("p (q c i r) -> p c i q r", q=G4, c=KT, i=NI)[:, half]
                                    hi, lo = (wall[:, bass.ds((2 * k + a) * n + half * NI * P, NI * P)].rearrange(
                                        "p (i q r) -> p i q r", i=NI, q=G4) for a in range(2))
                                else:
                                    s = src
                                    hi, lo = (wall[:, bass.ds((2 * k + a) * n, n)] for a in range(2))
                                if part == 0:
                                    last = nc.gpsimd.tensor_copy(hi, s)
                                else:
                                    last = nc.gpsimd.tensor_tensor(lo, s, hi, ALU.subtract)
                            last.then_inc(split_done, 1)
                            pool.wait_ge(split_done, 3 * k + 2 + part)

                    AFTER = NT - 3 * NM
                    with nc.gpsimd.Fori(0, AFTER - 1, 2) as j:
                        mask(j, 0)
                        mask(j + 1, 1)
                    pool.wait_ge(wmax_done, 3)
                    pool.wait_ge(masked, 2 * AFTER)
                    nc.gpsimd.partition_all_reduce(wmax_all[:, :], wmax[:, :], P, RMAX).then_inc(wmax_shared, 1)
                    pool.wait_ge(wmax_shared, 1)
                    mask(AFTER, 0)
                    mask(AFTER + 1, 1)
                    mask(AFTER + 2, 0)
                    mask(AFTER + 3, 1)
                    pool.wait_ge(scale_step, 4)
                    pool.wait_ge(masked, 2 * (AFTER + 4))
                    with nc.gpsimd.Fori(0, 2 * NM - 1, 2) as k:
                        split(k, True)
                        mask(k + AFTER + 4, 0)
                        pool.wait_ge(masked, 2 * (k + AFTER + 5))
                        split(k + 1, True)
                        mask(k + AFTER + 5, 1)
                        pool.wait_ge(masked, 2 * (k + AFTER + 6))
                    with nc.gpsimd.Fori(2 * NM, 3 * NM - 5, 2) as k:
                        split(k, False)
                        mask(k + AFTER + 4, 0)
                        pool.wait_ge(masked, 2 * (k + AFTER + 5))
                        split(k + 1, False)
                        mask(k + AFTER + 5, 1)
                        pool.wait_ge(masked, 2 * (k + AFTER + 6))
                    with nc.gpsimd.Fori(3 * NM - 4, 3 * NM) as k:
                        split(k, False)

        late = ExitStack()
        with late:
            xh = sbuf(late, "xh", [P, KT, T], F16)
            xl = sbuf(late, "xl", [P, KT, T], F16)
            wT = sbuf(late, "wT", [3 * E, T], BF16)
            with ExitStack() as phase:
                xn2 = [sbuf(phase, f"xn2_{i}", [P, D], F32) for i in range(2)]
                xTf = [sbuf(phase, f"xTf{i}", [P, KT, P], F32) for i in range(2)]
                lg = sbuf(phase, "lg", [P, NT, E], F32)
                lr = sbuf(phase, "lr", [P, NT, E], F32)
                ex = sbuf(phase, "ex", [P, NT, E], F32)
                mk = sbuf(phase, "mk", [P, NT, E], BF16)
                cum = sbuf(phase, "cum", [P, NT, E], BF16)
                w3 = sbuf(phase, "w3", [P, NT, 3, E], BF16)
                top = sbuf(phase, "top", [P, NT, TOP_K], F32)
                lmax = sbuf(phase, "lmax", [P, NT], F32)
                den = sbuf(phase, "den", [P, NT], F32)
                x_ps = [psum(phase, f"x_ps{i}", [P, 512], F32) for i in range(2)]
                lg_ps = psum(phase, "lg_ps", [P, NT, E], F32)
                pos_ps = psum(phase, "pos_ps", [P, NT, E], F32)
                wT_ps = psum(phase, "wT_ps", [P, 2, 8 * P], BF16)

                n2_done, t2_done, f_done, hi_done, lo_done, lg_done = (sem(n) for n in (
                    "n2_done", "t2_done", "f_done", "hi_done", "lo_done", "lg_done"))
                r_step, e_done, cum_done, pos_done, w3_done, wt_done, wt_copied = (sem(n) for n in (
                    "r_step", "e_done", "cum_done", "pos_done", "w3_done", "wt_done", "wt_copied"))

                def by_two(engine, step):
                    step(0, 0)
                    step(1, 1)
                    with engine.Fori(2, NT - 1, 2) as t:
                        step(t, 0)
                        step(t + 1, 1)

                with nc.Block() as block:
                    @block.vector
                    def _(dve):
                        def norm(t, b):
                            wait(dve, t2_done, t - 1)
                            nc.vector.tensor_scalar(xn2[b][:, :], xs[:, bass.ds(t, 1), :], mean[:, bass.ds(t, 1)],
                                                    rstd[:, bass.ds(t, 1)], ALU.subtract, ALU.mult
                                                    ).then_inc(n2_done, 1)

                        def lo(t, b):
                            wait(dve, hi_done, t + 1)
                            at = bass.ds(t * P, P)
                            nc.vector.tensor_tensor(xl[:, :, at], x_ps[b][:, 0:KT * P].rearrange("p (c n) -> p c n", c=KT),
                                                    xh[:, :, at], ALU.subtract).then_inc(lo_done, 1)

                        norm(0, 0)
                        norm(1, 1)
                        with nc.vector.Fori(0, NT - 3, 2) as t:
                            norm(t + 2, 0)
                            lo(t, 0)
                            norm(t + 3, 1)
                            lo(t + 1, 1)
                        lo(NT - 2, 0)
                        lo(NT - 1, 1)

                        count = [0]

                        def step(instruction):
                            count[0] += 1
                            instruction.then_inc(r_step, 1)
                            dve.wait_ge(r_step, count[0])

                        def over_e(v):
                            return v[:, :, None].to_broadcast([P, NT, E])

                        dve.wait_ge(lg_done, NT)
                        step(nc.vector.tensor_reduce(lmax[:, :], lg_ps[:, :, :], AX.X, ALU.max))
                        step(nc.vector.tensor_tensor(lg[:, :, :], lg_ps[:, :, :], over_e(lmax), ALU.subtract))
                        step(nc.vector.tensor_scalar(lg[:, :, :], lg[:, :, :], EXP_FLOOR, None, ALU.max))
                        for t in range(NT):
                            last = nc.vector.max(top[:, t, :], lg[:, t, :])
                        step(last)
                        for t in range(NT):
                            last = nc.vector.match_replace(lr[:, t, :], top[:, t, :], lg[:, t, :], -1e30)
                        step(last)
                        step(nc.vector.tensor_tensor(mk[:, :, :], lr[:, :, :], lg[:, :, :], ALU.not_equal))
                        dve.wait_ge(e_done, 1)
                        step(nc.vector.tensor_tensor(ex[:, :, :], ex[:, :, :], mk[:, :, :], ALU.mult))
                        step(nc.vector.tensor_reduce(den[:, :], ex[:, :, :], AX.X, ALU.add))
                        step(nc.vector.reciprocal(den[:, :], den[:, :]))
                        step(nc.vector.tensor_tensor(ex[:, :, :], ex[:, :, :], over_e(den), ALU.mult))
                        dve.wait_ge(pos_done, 1)
                        step(nc.vector.scalar_tensor_tensor(ex[:, :, :], pos_ps[:, :, :], float(CAP), ex[:, :, :],
                                                            ALU.is_lt, ALU.mult))
                        step(nc.vector.tensor_scalar(ex[:, :, :], ex[:, :, :], wfac[:, 0:1], None, ALU.mult))
                        for part in range(3):
                            step(nc.vector.tensor_copy(w3[:, :, part, :], ex[:, :, :]))
                            if part < 2:
                                step(nc.vector.tensor_tensor(ex[:, :, :], ex[:, :, :], w3[:, :, part, :],
                                                             ALU.subtract))
                        nc.vector.engine_nop().then_inc(w3_done, 1)
                        for i in range(4):
                            dve.wait_ge(wt_done, i + 1)
                            nc.vector.tensor_copy(wT[:, i * 8 * P:(i + 1) * 8 * P], wT_ps[0:3 * E, i % 2, :]
                                                  ).then_inc(wt_copied, 1)
                        dve.wait_ge(wt_copied, 4)

                    @block.tensor
                    def _(pe):
                        def transpose(t, b):
                            wait(pe, n2_done, t + 1)
                            wait(pe, f_done, t - 1)
                            wait(pe, lo_done, t - 1)
                            for c in range(KT):
                                last = nc.tensor.transpose(x_ps[b][:, c * P:(c + 1) * P],
                                                           xn2[b][:, c * P:(c + 1) * P], identf[:, :])
                            last.then_inc(t2_done, 1)

                        def gate(t, b):
                            wait(pe, f_done, t + 1)
                            for c in range(KT):
                                last = nc.tensor.matmul(lg_ps[:, bass.ds(t, 1), :], xTf[b][:, c, :], gatew[:, c, :],
                                                        start=(c == 0), stop=(c == KT - 1))
                            last.then_inc(lg_done, 1)

                        transpose(0, 0)
                        transpose(1, 1)
                        gate(0, 0)
                        transpose(2, 0)
                        gate(1, 1)
                        with nc.tensor.Fori(2, NT - 3, 2) as t:
                            transpose(t + 1, 1)
                            gate(t, 0)
                            transpose(t + 2, 0)
                            gate(t + 1, 1)
                        transpose(NT - 1, 1)
                        gate(NT - 2, 0)
                        gate(NT - 1, 1)
                        pe.wait_ge(r_step, 6)
                        pe.wait_ge(cum_done, NT)
                        half = NT // 2
                        for i in range(2):
                            at = slice(i * half, (i + 1) * half)
                            nc.tensor.matmul(pos_ps[:, at, :], tri[:, :], mk[:, at, :], start=True, stop=False)
                            last = nc.tensor.matmul(pos_ps[:, at, :], onesb[:, :], cum[:, at, :],
                                                    start=False, stop=True)
                        last.then_inc(pos_done, 1)
                        pe.wait_ge(w3_done, 1)
                        for i in range(4):
                            if i >= 2:
                                pe.wait_ge(wt_copied, i - 1)
                            for t in range(8):
                                last = nc.tensor.transpose(
                                    wT_ps[0:3 * E, i % 2, t * P:(t + 1) * P],
                                    w3[:, i * 8 + t, :, :].rearrange("p a e -> p (a e)"), identb[:, :])
                            last.then_inc(wt_done, 1)

                    @block.scalar
                    def _(act):
                        def copies(t, b):
                            wait(act, t2_done, t + 1)
                            wait(act, lg_done, t - 1)
                            src = x_ps[b][:, 0:KT * P].rearrange("p (c n) -> p c n", c=KT)
                            nc.scalar.activation(xTf[b][:, :, :], src, ACT.Copy).then_inc(f_done, 1)
                            nc.scalar.activation(xh[:, :, bass.ds(t * P, P)], src, ACT.Copy).then_inc(hi_done, 1)
                        by_two(nc.scalar, copies)
                        act.wait_ge(r_step, 3)
                        nc.scalar.activation(ex[:, :, :], lg[:, :, :], ACT.Exp).then_inc(e_done, 1)

                    @block.gpsimd
                    def _(pool):
                        nc.gpsimd.memset(cum[:, 0, :], 0.0).then_inc(cum_done, 1)
                        pool.wait_ge(r_step, 6)
                        for t in range(1, NT):
                            pool.wait_ge(cum_done, t)
                            nc.gpsimd.tensor_tensor(cum[:, t, :], cum[:, t - 1, :], mk[:, t - 1, :], ALU.add
                                                    ).then_inc(cum_done, 1)

            with ExitStack() as phase:
                NS = (T // NB) * (NM // 2)
                SPB = NM // 2
                CH = 2 * NI
                ysum = sbuf(phase, "ysum", [P, KT, T], F32)
                sg = [sbuf(phase, f"sg{i}", [P, NB], F32) for i in range(2)]
                wb = [sbuf(phase, f"wb{i}", [P, NB], F32) for i in range(2)]
                hf = [sbuf(phase, f"hf{i}", [P, NB], F32) for i in range(2)]
                yt = [sbuf(phase, f"yt{i}", [P, KT, P], F32) for i in range(2)]
                hh = [sbuf(phase, f"hh{i}", [P, NB], F16) for i in range(NI)]
                hl = [sbuf(phase, f"hl{i}", [P, NB], F16) for i in range(NI)]
                g_ps = [psum(phase, f"g_ps{i}", [P, NB], F32) for i in range(2)]
                u_ps = [psum(phase, f"u_ps{i}", [P, NB], F32) for i in range(2)]
                b_ps = psum(phase, "b_ps", [P, NB], F32)
                f_ps = psum(phase, "f_ps", [P, NB], F32)
                y_ps = psum(phase, "y_ps", [P, KT, NB], F32)

                gu_done, silu_done, wb_made, wb_copied, sgw_done = (sem(n) for n in (
                    "gu_done", "silu_done", "wb_made", "wb_copied", "sgw_done"))
                h_done, hh_done, hl_done, down_done, y_added = (sem(n) for n in (
                    "h_done", "hh_done", "hl_done", "down_done", "y_added"))
                yt_done, ft_done, fin_done, stored = sem("yt_done"), sem("ft_done"), sem("fin_done"), sem("stored")

                def over_steps(engine, step, start, end):
                    with engine.Fori(start, end) as s:
                        step(s)

                def block_of(s):
                    return s // SPB if isinstance(s, int) else nc.s_assert_within(
                        s >> 2, 0, T // NB - 1, skip_runtime_bounds_check_because="the loop ends at NS")

                def pair_of(s):
                    return s % SPB if isinstance(s, int) else nc.s_assert_within(
                        s & 3, 0, SPB - 1, skip_runtime_bounds_check_because="the loop ends at NS")

                with nc.Block() as block:
                    @block.tensor
                    def _(pe):
                        def spread(s, a):
                            m = 2 * s + a
                            wait(pe, wb_copied, m)
                            nc.tensor.matmul(b_ps[:, :], sel[:, bass.ds(2 * pair_of(s) + a, 1), :],
                                             wT[:, bass.ds(block_of(s) * NB, NB)], start=True, stop=True
                                             ).then_inc(wb_made, 1)

                        def gate_up(s, j):
                            c = CH * s + j
                            wait(pe, silu_done, c - 1)
                            wait(pe, h_done, c - 1)
                            tok = block_of(s) * NB
                            for n, dst in ((0, g_ps), (1, u_ps)):
                                base = (pair_of(s) * 2 + (n * NM + j // NI)) * (2 * SLOT) + (j % NI) * P
                                terms = [(part, xp, half) for half in range(KT) for part, xp in
                                         ((0, xh), (0, xl), (1, xh))]
                                for i, (part, xp, half) in enumerate(terms):
                                    last = nc.tensor.matmul(
                                        dst[j % 2][:, :], wall[:, bass.ds(base + part * SLOT + half * NI * P, P)],
                                        xp[:, half, bass.ds(tok, NB)], start=(i == 0), stop=(i == len(terms) - 1))
                            last.then_inc(gu_done, 1)

                        def down(s, j):
                            c = CH * s + j
                            wait(pe, hl_done, c + 1)
                            if j == 0:
                                wait(pe, y_added, s + 1)
                            base = (pair_of(s) * 2 + (2 * NM + j // NI)) * (2 * SLOT) + (j % NI) * D
                            for half in range(KT):
                                for i, (part, hp) in enumerate(((0, hh), (0, hl), (1, hh))):
                                    last = nc.tensor.matmul(
                                        y_ps[:, half, :], wall[:, bass.ds(base + part * SLOT + half * P, P)],
                                        hp[j % NI][:, :], start=(j == 0 and i == 0), stop=(j == CH - 1 and i == 2))
                            last.then_inc(down_done, 1)

                        def step(s):
                            gate_up(s, 2)
                            down(s, 0)
                            spread(s, 1)
                            gate_up(s, 3)
                            down(s, 1)
                            gate_up(s, 4)
                            down(s, 2)
                            gate_up(s, 5)
                            down(s, 3)

                        spread(0, 0)
                        gate_up(0, 0)
                        gate_up(0, 1)
                        with nc.tensor.Fori(0, NS - 1) as s:
                            step(s)
                            spread(s + 1, 0)
                            gate_up(s + 1, 0)
                            down(s, 4)
                            gate_up(s + 1, 1)
                            down(s, 5)
                        step(NS - 1)
                        down(NS - 1, 4)
                        down(NS - 1, 5)

                    @block.scalar
                    def _(act):
                        def copy_wb(s, a):
                            wait(act, wb_made, 2 * s + a + 1)
                            wait(act, sgw_done, CH * (s - 1) + NI * (a + 1))
                            nc.scalar.activation(wb[a][:, :], b_ps[:, :], ACT.Copy).then_inc(wb_copied, 1)

                        def silu(s, j):
                            c = CH * s + j
                            wait(act, gu_done, c + 1)
                            wait(act, h_done, c - 1)
                            nc.scalar.activation(sg[j % 2][:, :], g_ps[j % 2][:, :], ACT.Silu, scale=pow2[:, 0:1]
                                                 ).then_inc(silu_done, 1)

                        def hi(s, j):
                            c = CH * s + j
                            wait(act, h_done, c + 1)
                            wait(act, down_done, c - 2)
                            nc.scalar.activation(hh[j % NI][:, :], hf[j % 2][:, :], ACT.Copy).then_inc(hh_done, 1)

                        def step(s, first=False):
                            for j in range(CH):
                                if j % NI == 0:
                                    copy_wb(s, j // NI)
                                silu(s, j)
                                if j:
                                    hi(s, j - 1)
                            hi(s, CH - 1)
                        step(0)
                        over_steps(nc.scalar, step, 1, NS)

                    @block.gpsimd
                    def _(pool):
                        nc.gpsimd.memset(ysum[:, :, :], 0.0).then_inc(y_added, 1)

                        def step(s):
                            for j in range(CH):
                                c = CH * s + j
                                pool.wait_ge(silu_done, c + 1)
                                if j % NI == 0:
                                    pool.wait_ge(wb_copied, 2 * s + j // NI + 1)
                                nc.gpsimd.tensor_tensor(sg[j % 2][:, :], sg[j % 2][:, :], wb[j // NI][:, :], ALU.mult
                                                        ).then_inc(sgw_done, 1)
                        over_steps(nc.gpsimd, step, 0, NS)

                    @block.vector
                    def _(dve):
                        def hidden(s, j):
                            c = CH * s + j
                            wait(dve, sgw_done, c + 1)
                            wait(dve, hl_done, c - 1)
                            nc.vector.tensor_tensor(hf[j % 2][:, :], sg[j % 2][:, :], u_ps[j % 2][:, :], ALU.mult
                                                    ).then_inc(h_done, 1)

                        def lo(s, j):
                            c = CH * s + j
                            wait(dve, hh_done, c + 1)
                            wait(dve, down_done, c - 2)
                            nc.vector.tensor_tensor(hl[j % NI][:, :], hf[j % 2][:, :], hh[j % NI][:, :], ALU.subtract
                                                    ).then_inc(hl_done, 1)

                        def add(s):
                            wait(dve, down_done, CH * (s + 1))
                            wait(dve, y_added, s + 1)
                            v = ysum[:, :, bass.ds(block_of(s) * NB, NB)]
                            nc.vector.tensor_tensor(v, v, y_ps[:, :, :], ALU.add).then_inc(y_added, 1)

                        def step(s, before):
                            hidden(s, 0)
                            lo(s, 0)
                            hidden(s, 1)
                            lo(s, 1)
                            if before:
                                add(s - 1)
                            for j in range(2, CH):
                                hidden(s, j)
                                lo(s, j)
                        step(0, False)
                        with nc.vector.Fori(1, NS) as s:
                            step(s, True)
                        add(NS - 1)
                        dve.wait_ge(y_added, NS + 1)

                with nc.Block() as block:
                    @block.scalar
                    def _(act):
                        def step(t, b):
                            wait(act, ft_done, t - 1)
                            nc.scalar.activation(yt[b][:, :, :], ysum[:, :, bass.ds(t * P, P)], ACT.Copy
                                                 ).then_inc(yt_done, 1)
                        by_two(nc.scalar, step)

                    @block.tensor
                    def _(pe):
                        def step(t, b):
                            wait(pe, yt_done, t + 1)
                            wait(pe, fin_done, t - 1)
                            for c in range(KT):
                                last = nc.tensor.transpose(g_ps[b][:, c * P:(c + 1) * P],
                                                           yt[b][:, c, :], identf[:, :])
                            last.then_inc(ft_done, 1)
                        by_two(nc.tensor, step)

                    @block.vector
                    def _(dve):
                        def step(t, b):
                            wait(dve, ft_done, t + 1)
                            row = xs[:, bass.ds(t, 1), :]
                            nc.vector.scalar_tensor_tensor(row, g_ps[b][:, 0:D][:, None, :], yfac[:, 0:1], row,
                                                           ALU.mult, ALU.add).then_inc(fin_done, 1)
                        by_two(nc.vector, step)

                    @block.sync
                    def _(sp):
                        n = 4
                        with nc.sync.Fori(0, NT // n) as i:
                            sp.wait_ge(fin_done, i * n + n)
                            sp.dma_start(out_rows[bass.ds(i * (n * P), n * P), :].rearrange("(t p) d -> p t d", p=P),
                                         xs[:, bass.ds(i * n, n), :]).then_inc(stored, 16)
                        sp.wait_ge(stored, 16 * (NT // n))


_INS = ['x', 'ctx_2048', 'g_xattn', 'g_ffn', 'L0_ffn_gate_w', 'L0_ffn_w_gate', 'L0_ffn_w_up', 'L0_ffn_w_down']


def kernel(**inputs):
    import numpy as _np
    import concourse.bacc as _bacc
    from concourse import mybir as _mybir
    from concourse.bass_utils import run_bass_kernel_spmd as _run

    nc = _bacc.Bacc("TRN2", target_bir_lowering=False, num_devices=1)
    arrays, args = {}, []
    for name in _INS:
        a = _np.ascontiguousarray(inputs[name])
        arrays[f"in_{name}_dram"] = a
        args.append(nc.dram_tensor(f"in_{name}_dram", a.shape, _mybir.dt.from_np(a.dtype), kind="ExternalInput").ap())
    args.append(nc.dram_tensor("out_0_dram", arrays["in_x_dram"].shape, _mybir.dt.float32, kind="ExternalOutput").ap())
    build(nc, *args)
    r = _run(nc, [arrays], core_ids=[0])
    return r.results[0]["out_0_dram"]
```

```python
from contextlib import ExitStack

import concourse.bass as bass
from concourse import mybir

P = 128
F32 = mybir.dt.float32
F16 = mybir.dt.float16
BF16 = mybir.dt.bfloat16
I32 = mybir.dt.int32
ALU = mybir.AluOpType
ACT = mybir.ActivationFunctionType
AX = mybir.AxisListType
RMAX = bass.bass_isa.ReduceOp.max

HEADS = 16
TOP_K = 8
EPS = 1e-5
MASKED = -10000.0
EXP_FLOOR = -104.0


def build(nc, x, ctx_in, g_xattn, g_ffn, gate_w, w_gate, w_up, w_down, out):
    B, S, D = x.shape
    E, _, INTER = w_gate.shape
    T = B * S
    NT = T // P
    HD = D // HEADS
    KT = D // P
    CAP = 2 * (T * TOP_K // E)
    G4 = P // 32
    NM = E // G4
    NI = INTER // 32
    NB = 512
    TPB = NB // P
    AHEAD = 5
    SLOT = NI * P * KT
    assert S == 64 and HD == 16 and KT == 2 and SLOT == NI * D

    x_rows = x.rearrange("b s d -> (b s) d")
    ctx_rows = ctx_in.rearrange("b s d -> (b s) d")
    out_rows = out.rearrange("b s d -> (b s) d")

    persist = ExitStack()

    def sbuf(stack, name, shape, dt):
        return stack.enter_context(nc.sbuf_tensor(name, shape, dt))

    def psum(stack, name, shape, dt):
        return stack.enter_context(nc.psum_tensor(name, shape, dt))

    def sem(name):
        return persist.enter_context(nc.semaphore(name))

    with persist:
        xs = sbuf(persist, "xs", [P, NT, D], F32)
        wall = sbuf(persist, "wall", [P, (3 * NM + 1) * SLOT * 2], F16)
        wall32 = wall[:, :].bitcast(F32)
        gatew = sbuf(persist, "gatew", [P, KT, E], F32)
        identf = sbuf(persist, "identf", [P, P], F32)
        identb = sbuf(persist, "identb", [P, P], BF16)
        tri = sbuf(persist, "tri", [P, P], BF16)
        onesb = sbuf(persist, "onesb", [P, P], BF16)
        sel = sbuf(persist, "sel", [3 * E, NM, P], BF16)
        parity = sbuf(persist, "parity", [P, 2], F32)
        gates = sbuf(persist, "gates", [P, 2], F32)
        tanhg = sbuf(persist, "tanhg", [P, 2], F32)
        stats = sbuf(persist, "stats", [P, NT, 6], F32)
        mean = sbuf(persist, "mean", [P, NT], F32)
        rstd = sbuf(persist, "rstd", [P, NT], F32)
        va = sbuf(persist, "va", [P, NT], F32)
        vb = sbuf(persist, "vb", [P, NT], F32)
        wmax = sbuf(persist, "wmax", [P, 3], F32)
        wmax_all = sbuf(persist, "wmax_all", [P, 3], F32)
        pow2 = sbuf(persist, "pow2", [P, 3], F32)
        inv2 = sbuf(persist, "inv2", [P, 3], F32)
        inv24 = sbuf(persist, "inv24", [P, 3 * NM], F32)
        wfac = sbuf(persist, "wfac", [P, 1], F32)
        yfac = sbuf(persist, "yfac", [P, 1], F32)

        x_in = [sem(f"x_in{i}") for i in range(4)]
        small_in = sem("small_in")
        w_in = [sem(f"w_in{i}") for i in range(3)]
        zeros_set, masks_set = sem("zeros_set"), sem("masks_set")
        tanh_done = sem("tanh_done")
        stat_step = sem("stat_step")
        sqrt_done = sem("sqrt_done")
        wmax_done, wmax_shared, scale_step = sem("wmax_done"), sem("wmax_shared"), sem("scale_step")

        def finish_stats(dve, base):
            me, m2e, mo, m2o = (stats[:, :, k] for k in (1, 2, 4, 5))
            count = [base]

            def step(instruction):
                count[0] += 1
                instruction.then_inc(stat_step, 1)
                dve.wait_ge(stat_step, count[0])

            step(nc.vector.tensor_tensor(va[:, :], me, mo, ALU.subtract))
            step(nc.vector.tensor_tensor(mean[:, :], me, mo, ALU.add))
            step(nc.vector.tensor_tensor(vb[:, :], m2e, m2o, ALU.add))
            step(nc.vector.tensor_scalar(mean[:, :], mean[:, :], 0.5, None, ALU.mult))
            step(nc.vector.scalar_tensor_tensor(va[:, :], va[:, :], 0.25, va[:, :], ALU.mult, ALU.mult))
            step(nc.vector.tensor_scalar(vb[:, :], vb[:, :], 1.0 / D, EPS, ALU.mult, ALU.add))
            step(nc.vector.tensor_tensor(vb[:, :], vb[:, :], va[:, :], ALU.add))
            return count[0]

        def finish_rstd(dve, base, which):
            count = [base]

            def step(instruction):
                count[0] += 1
                instruction.then_inc(stat_step, 1)
                dve.wait_ge(stat_step, count[0])

            dve.wait_ge(sqrt_done, which)
            step(nc.vector.reciprocal(rstd[:, :], va[:, :]))
            step(nc.vector.tensor_tensor(va[:, :], rstd[:, :], rstd[:, :], ALU.mult))
            step(nc.vector.tensor_tensor(va[:, :], va[:, :], vb[:, :], ALU.mult))
            step(nc.vector.tensor_scalar(va[:, :], va[:, :], -0.5, 1.5, ALU.mult, ALU.add))
            step(nc.vector.tensor_tensor(rstd[:, :], rstd[:, :], va[:, :], ALU.mult))
            return count[0]

        STATS = 7
        RSTD = 5

        with nc.Block() as block:
            @block.sync
            def _(sp):
                for i in range(4):
                    n = NT // 4
                    sp.dma_start(xs[:, i * n:(i + 1) * n, :],
                                 x_rows[i * n * P:(i + 1) * n * P, :].rearrange("(t p) d -> p t d", p=P)
                                 ).then_inc(x_in[i], 16)
                sp.dma_start(gatew[:, :, :], gate_w.rearrange("(k p) e -> p k e", p=P)).then_inc(small_in, 16)
                for i, g in enumerate((g_xattn, g_ffn)):
                    sp.dma_start(gates[:, i:i + 1], g.rearrange("(a b) -> a b", b=1).to_broadcast([P, 1])
                                 ).then_inc(small_in, 16)

            @block.gpsimd
            def _(pool):
                nc.gpsimd.memset(identf[:, :], 0.0).then_inc(zeros_set, 1)
                nc.gpsimd.memset(identb[:, :], 0.0).then_inc(zeros_set, 1)
                nc.gpsimd.memset(tri[:, :], 1.0).then_inc(zeros_set, 1)
                nc.gpsimd.memset(sel[:, :, :], 0.0).then_inc(zeros_set, 1)
                nc.gpsimd.memset(parity[:, :], 1.0).then_inc(zeros_set, 1)
                nc.gpsimd.memset(onesb[:, :], 1.0).then_inc(zeros_set, 1)
                pool.wait_ge(zeros_set, 6)
                made = [0]

                def mask(v, compare, fill, base, pattern, per_row):
                    nc.gpsimd.affine_select(out=v, in_=v, compare_op=compare, fill=fill, base=base, pattern=pattern,
                                            channel_multiplier=per_row).then_inc(masks_set, 1)
                    made[0] += 1
                    pool.wait_ge(masks_set, made[0])

                for m in (identf, identb):
                    mask(m[:, :], ALU.not_equal, 1.0, 0, [[-1, P]], 1)
                mask(tri[:, :], ALU.is_gt, 0.0, 0, [[1, P]], -1)
                for part in range(3):
                    mask(sel[part * E:(part + 1) * E, :, :].rearrange("p m (q r) -> p m q r", q=G4),
                         ALU.not_equal, 1.0, 0, [[-G4, NM], [-1, G4], [0, 32]], 1)
                for g in range(G4):
                    even, odd = (parity[32 * g:32 * g + 32, h:h + 1] for h in range(2))
                    mask(even, ALU.is_ge, 0.0, HD - 1, [[0, 1]], -1)
                    mask(odd, ALU.is_ge, 0.0, -HD, [[0, 1]], 1)

            @block.vector
            def _(dve):
                for i in range(4):
                    dve.wait_ge(x_in[i], 16)
                    with nc.vector.Fori(i * NT // 4, (i + 1) * NT // 4) as t:
                        nc.vector.bn_stats(stats[:, bass.ds(t, 1), :], xs[:, bass.ds(t, 1), :]).then_inc(stat_step, 1)
                dve.wait_ge(stat_step, NT)
                finish_stats(dve, NT)
                finish_rstd(dve, NT + STATS, 1)

            @block.scalar
            def _(act):
                act.wait_ge(stat_step, NT + STATS)
                nc.scalar.activation(va[:, :], vb[:, :], ACT.Sqrt).then_inc(sqrt_done, 1)
                act.wait_ge(small_in, 48)
                nc.scalar.activation(tanhg[:, :], gates[:, :], ACT.Tanh).then_inc(tanh_done, 1)
                act.wait_ge(tanh_done, 1)

        with ExitStack() as phase:
            cnat = [sbuf(phase, f"cnat{i}", [P, D], F32) for i in range(2)]
            cdup = [sbuf(phase, f"cdup{i}", [P, 2, D], F32) for i in range(2)]
            xn = [sbuf(phase, f"xn{i}", [P, D], F32) for i in range(2)]
            qT = [sbuf(phase, f"qT{i}", [P, KT, P], F32) for i in range(2)]
            kpair = [sbuf(phase, f"kpair{i}", [P, KT * 2, 2, S], F32) for i in range(2)]
            sc = [sbuf(phase, f"sc{i}", [P, HEADS, S], F32) for i in range(2)]
            pr = [sbuf(phase, f"pr{i}", [P, HEADS * S], F32) for i in range(2)]
            pT = [sbuf(phase, f"pT{i}", [P, HEADS // 2, P], F32) for i in range(2)]
            vpair = [sbuf(phase, f"vpair{i}", [P, 2, HEADS // 2, 2, HD], F32) for i in range(2)]
            oT = [sbuf(phase, f"oT{i}", [P, KT, P], F32) for i in range(2)]
            smax = sbuf(phase, "smax", [P, HEADS], F32)
            den = [sbuf(phase, f"den{i}", [P, HEADS], F32) for i in range(2)]
            rden = [sbuf(phase, f"rden{i}", [P, HEADS], F32) for i in range(2)]
            att = sbuf(phase, "att", [P, HEADS, HD], F32)
            qk_ps = psum(phase, "qk_ps", [P, 2 * KT, P], F32)
            s_ps = psum(phase, "s_ps", [P, G4, 512], F32)
            pT_ps = psum(phase, "pT_ps", [P, HEADS // 2, P], F32)
            o_ps = psum(phase, "o_ps", [P, 2, KT * P], F32)
            oT_ps = o_ps[:, 0, :].rearrange("p (c n) -> p c n", c=KT)
            cnat_in = [sem(f"cnat_in{i}") for i in range(2)]
            cdup_in = [sem(f"cdup_in{i}") for i in range(2)]
            ln_done, tqk_done, q_done, k_done = sem("ln_done"), sem("tqk_done"), sem("q_done"), sem("k_done")
            s_done, s_copied, masked, max_done, sub_done = (sem(n) for n in (
                "s_done", "s_copied", "masked", "max_done", "sub_done"))
            exp_done, tp_done, pT_done, v_done = (sem(n) for n in (
                "exp_done", "tp_done", "pT_done", "v_done"))
            rden_step, att_done, x1_done, v_init = sem("rden_step"), sem("att_done"), sem("x1_done"), sem("v_init")
            mask_turn, den_done, oT_made, oT_done, o_done = (sem(n) for n in (
                "mask_turn", "den_done", "oT_made", "oT_done", "o_done"))
            scaled, hi_split, lo_split = sem("scaled"), sem("hi_split"), sem("lo_split")

            FIRST, LAST = -4, NT + 4
            LOOP = (6, NT - 4)
            HI_AT = 10

            def pipeline(engine, step, first=FIRST, last=LAST, loop=LOOP):
                for n in range(first, loop[0]):
                    step(n, n)
                with engine.Fori(loop[0], loop[1] - 1, 2) as n:
                    step(n, 0)
                    step(n + 1, 1)
                for n in range(loop[1], last):
                    step(n, n)

            def has(j):
                return not isinstance(j, int) or 0 <= j < NT

            def wait(engine, s, count):
                if not isinstance(count, int) or count > 0:
                    engine.wait_ge(s, count)

            def piece(k, expand):
                n = SLOT
                src = wall32[:, bass.ds((k + 1) * n, n)]
                if not expand:
                    return [src], *([wall[:, bass.ds((2 * k + a) * n, n)]] for a in range(2))
                src = src.rearrange("p (q c i r) -> p c i q r", q=G4, c=KT, i=NI)
                return [src[:, c] for c in range(KT)], *([wall[:, bass.ds((2 * k + a) * n + c * NI * P, NI * P)]
                                                          .rearrange("p (i q r) -> p i q r", i=NI, q=G4)
                                                          for c in range(KT)] for a in range(2))

            def landed(j, b, per):
                return (j - b) * 8 * per + 16 * per

            with nc.Block() as block:
                @block.sync
                def _(sp):
                    def step(n, k):
                        j, b = n + 4, k % 2
                        if has(j):
                            wait(sp, tqk_done, j - 1)
                            sp.dma_start(cnat[b][:, :], ctx_rows[bass.ds(j * P, P), :]).then_inc(cnat_in[b], 16)
                        j, b = n, k % 2
                        if has(j):
                            wait(sp, v_done, j - 1)
                            src = ctx_rows[bass.ds(j * P, P), :].rearrange("(b s) d -> s b d", b=2)
                            for half in range(2):
                                sp.dma_start(cdup[b][64 * half:64 * half + 64, :, :], src).then_inc(cdup_in[b], 16)
                    pipeline(nc.sync, step)

                @block.tensor
                def _(pe):
                    def step(n, k):
                        j, b = n + 1, (k + 1) % 2
                        if has(j):
                            wait(pe, ln_done, j + 1)
                            wait(pe, cnat_in[b], landed(j, b, 1))
                            wait(pe, q_done, j)
                            for c in range(KT):
                                nc.tensor.transpose(qk_ps[:, c, :], xn[b][:, c * P:(c + 1) * P], identf[:, :])
                            for c in range(KT):
                                last = nc.tensor.transpose(qk_ps[:, KT + c, :], cnat[b][:, c * P:(c + 1) * P],
                                                           identf[:, :])
                            last.then_inc(tqk_done, 1)
                        j, b = n - 4, k % 2
                        if has(j):
                            wait(pe, oT_done, j + 1)
                            for c in range(KT):
                                last = nc.tensor.transpose(o_ps[:, 1, c * P:(c + 1) * P], oT[b][:, c, :], identf[:, :])
                            last.then_inc(o_done, 1)
                        j, b = n - 2, k % 2
                        if has(j):
                            wait(pe, exp_done, j + 1)
                            wait(pe, pT_done, j)
                            for c in range(HEADS // 2):
                                last = nc.tensor.transpose(pT_ps[:, c, :], pr[b][:, c * P:(c + 1) * P], identf[:, :])
                            last.then_inc(tp_done, 1)
                        j, b = n, k % 2
                        if has(j):
                            wait(pe, q_done, j + 1)
                            wait(pe, s_copied, j)
                            for c in range(KT):
                                for h in range(2):
                                    for g in range(G4):
                                        rows = slice(32 * g, 32 * g + 32)
                                        last = nc.tensor.matmul(
                                            s_ps[64 * h:64 * h + 64, g, c * P:(c + 1) * P],
                                            qT[b][rows, c, 64 * h:64 * h + 64],
                                            kpair[b][rows, 2 * c + h, :, :].rearrange("p a s -> p (a s)"),
                                            start=True, stop=True)
                            last.then_inc(s_done, 1)
                        j, b = n - 3, (k + 1) % 2
                        if has(j):
                            wait(pe, pT_done, j + 1)
                            wait(pe, v_done, j + 1)
                            wait(pe, att_done, j)
                            for h in range(2):
                                for pair in range(HEADS // 2):
                                    c, g = pair // G4, pair % G4
                                    last = nc.tensor.matmul(
                                        oT_ps[32 * g:32 * g + 32, c, 64 * h:64 * h + 64],
                                        vpair[b][:, h, pair, :, :].rearrange("p a d -> p (a d)"),
                                        pT[b][:, pair, 64 * h:64 * h + 64], start=True, stop=True)
                            last.then_inc(oT_made, 1)
                    pipeline(nc.tensor, step)

                @block.scalar
                def _(act):
                    for n, w in ((0, w_gate), (1, w_up)):
                        at = (1 + n * NM) * SLOT
                        act.dma_start(wall32[:, at:at + NM * SLOT].rearrange("p (a i) -> p a i", i=INTER),
                                     w.rearrange("e (k p) i -> p (e k) i", p=P)).then_inc(w_in[n], 16)
                    at = (1 + 2 * NM) * SLOT
                    for q in range(G4):
                        for i in range(NI):
                            act.dma_start(wall32[32 * q:32 * q + 32, at:at + NM * SLOT].rearrange(
                                "p (m i n) -> p i m n", m=NM, i=NI)[:, i],
                                w_down.rearrange("(m q) (i r) n -> q i r m n", q=G4, r=32)[q, i]).then_inc(w_in[2], 16)

                    def hi(k, expand):
                        act.wait_ge(scaled, k + 1)
                        wait(act, lo_split, k)
                        src, his, _ = piece(k, expand)
                        for s, h in zip(src, his):
                            last = nc.scalar.activation(h, s, ACT.Copy)
                        last.then_inc(hi_split, 1)

                    def step(n, k):
                        j, b = n - 2, k % 2
                        if has(j):
                            wait(act, sub_done, j + 1)
                            wait(act, tp_done, j - 1)
                            wait(act, den_done, j - 1)
                            nc.scalar.activation(pr[b][:, :], sc[b][:, :, :].rearrange("p h s -> p (h s)"),
                                                 ACT.Exp).then_inc(exp_done, 1)
                        j, b = n + 1, (k + 1) % 2
                        if has(j):
                            wait(act, k_done, j + 1)
                            wait(act, s_done, j - 1)
                            nc.scalar.activation(qT[b][:, :, :], qk_ps[:, 0:KT, :], ACT.Copy).then_inc(q_done, 1)
                        j, b = n - 2, k % 2
                        if has(j):
                            wait(act, tp_done, j + 1)
                            wait(act, oT_made, j - 1)
                            nc.scalar.activation(pT[b][:, :, :], pT_ps[:, :, :], ACT.Copy).then_inc(pT_done, 1)
                        j, b = n, k % 2
                        if has(j):
                            wait(act, s_done, j + 1)
                            wait(act, exp_done, j - 1)
                            src = s_ps[:, :, 0:2 * P].rearrange("p g (c n) -> p g c n", c=KT)
                            dst = sc[b][:, :, :].rearrange("p (c g a) s -> p g c (a s)", c=KT, g=G4)
                            nc.scalar.activation(dst, src, ACT.Copy, scale=HD ** -0.5).then_inc(s_copied, 1)
                        j, b = n - 3, (k + 1) % 2
                        if has(j):
                            wait(act, oT_made, j + 1)
                            wait(act, o_done, j - 1)
                            nc.scalar.activation(oT[b][:, :, :], oT_ps, ACT.Copy).then_inc(oT_done, 1)

                    def step_hi(n, k, expand):
                        step(n, k)
                        hi(n - HI_AT, expand)

                    for n in range(FIRST, LOOP[0]):
                        step(n, n)
                    with nc.scalar.Fori(LOOP[0], HI_AT - 1, 2) as n:
                        step(n, 0)
                        step(n + 1, 1)
                    with nc.scalar.Fori(HI_AT, HI_AT + 2 * NM - 1, 2) as n:
                        step_hi(n, 0, True)
                        step_hi(n + 1, 1, True)
                    for n in range(HI_AT + 2 * NM, LAST):
                        step(n, n)
                        if n - HI_AT < 3 * NM:
                            hi(n - HI_AT, False)
                    act.wait_ge(stat_step, NT + STATS + RSTD + NT + STATS)
                    nc.scalar.activation(va[:, :], vb[:, :], ACT.Sqrt).then_inc(sqrt_done, 1)

                @block.vector
                def _(dve):
                    for b in range(2):
                        last = nc.vector.memset(vpair[b][:, :, :, :, :], 0.0)
                    last.then_inc(v_init, 1)
                    dve.wait_ge(v_init, 1)

                    def step(n, k):
                        j, b = n + 1, (k + 1) % 2
                        if has(j):
                            wait(dve, tqk_done, j + 1)
                            wait(dve, s_done, j - 1)
                            nc.vector.tensor_tensor(
                                kpair[b][:, :, :, :],
                                qk_ps[:, KT:2 * KT, :].rearrange("p c (h s) -> p (c h) s", h=2)[:, :, None, :]
                                .to_broadcast([P, 2 * KT, 2, S]),
                                parity[:, None, :, None].to_broadcast([P, 2 * KT, 2, S]),
                                ALU.mult).then_inc(k_done, 1)
                        j, b = n + 2, k % 2
                        if has(j):
                            wait(dve, tqk_done, j - 1)
                            nc.vector.tensor_scalar(xn[b][:, :], xs[:, bass.ds(j, 1), :], mean[:, bass.ds(j, 1)],
                                                    rstd[:, bass.ds(j, 1)], ALU.subtract, ALU.mult
                                                    ).then_inc(ln_done, 1)
                        j, b = n - 2, k % 2
                        if has(j):
                            wait(dve, cdup_in[b], landed(j, b, 2))
                            wait(dve, oT_made, j - 1)
                            src = cdup[b][:, :, :].rearrange("p h (c a d) -> p h c a d", a=2, d=HD)
                            for half in range(2):
                                rows = slice(64 * half, 64 * half + 64)
                                last = nc.vector.tensor_copy(vpair[b][rows, :, :, half, 0:HD], src[rows, :, :, half, :])
                            last.then_inc(v_done, 1)
                        j, b = n - 4, k % 2
                        if has(j):
                            wait(dve, o_done, j + 1)
                            wait(dve, x1_done, j)
                            wait(dve, rden_step, 2 * j + 2)
                            nc.vector.tensor_tensor(att[:, :, :], o_ps[:, 1, :].rearrange("p (h d) -> p h d", d=HD),
                                                    rden[b][:, :, None].to_broadcast([P, HEADS, HD]),
                                                    ALU.mult).then_inc(att_done, 1)
                            wait(dve, att_done, j + 1)
                            row = xs[:, bass.ds(j, 1), :]
                            nc.vector.tensor_tensor(row, row, att[:, :, :].rearrange("p h d -> p (h d)")[:, None, :],
                                                    ALU.add).then_inc(x1_done, 1)
                            wait(dve, x1_done, j + 1)
                            nc.vector.bn_stats(stats[:, bass.ds(j, 1), :], row).then_inc(stat_step, 1)
                        j, b = n - 1, (k + 1) % 2
                        if has(j):
                            wait(dve, masked, 2 * j + 2)
                            wait(dve, sub_done, j)
                            nc.vector.tensor_reduce(smax[:, :], sc[b][:, :, :], AX.X, ALU.max).then_inc(max_done, 1)
                            wait(dve, max_done, j + 1)
                            nc.vector.tensor_tensor(sc[b][:, :, :], sc[b][:, :, :],
                                                    smax[:, :, None].to_broadcast([P, HEADS, S]),
                                                    ALU.subtract).then_inc(sub_done, 1)
                        j, b = n - 2, k % 2
                        if has(j):
                            wait(dve, exp_done, j + 1)
                            wait(dve, att_done, j - 1)
                            nc.vector.tensor_reduce(den[b][:, :], pr[b][:, :].rearrange("p (h s) -> p h s", s=S), AX.X,
                                                    ALU.add).then_inc(den_done, 1)
                            wait(dve, den_done, j + 1)
                            nc.vector.reciprocal(rden[b][:, :], den[b][:, :]).then_inc(rden_step, 1)
                            wait(dve, rden_step, 2 * j + 1)
                            nc.vector.tensor_scalar(rden[b][:, :], rden[b][:, :], tanhg[:, 0:1], None, ALU.mult
                                                    ).then_inc(rden_step, 1)

                    SPLIT = 8
                    for n in range(FIRST, LOOP[0]):
                        step(n, n)
                    with nc.vector.Fori(LOOP[0], SPLIT - 1, 2) as n:
                        step(n, 0)
                        step(n + 1, 1)
                    for i in range(3):
                        at = (1 + i * NM) * SLOT
                        dve.wait_ge(w_in[i], 16 if i < 2 else 16 * G4 * NI)
                        nc.vector.tensor_reduce(wmax[:, i:i + 1], wall32[:, at:at + NM * SLOT], AX.X, ALU.max,
                                                apply_absolute_value=True).then_inc(wmax_done, 1)
                    with nc.vector.Fori(SPLIT, SPLIT + 1, 2) as n:
                        step(n, 0)
                        step(n + 1, 1)
                    dve.wait_ge(wmax_shared, 1)
                    nc.vector.tensor_scalar(pow2[:, :].bitcast(I32), wmax_all[:, :].bitcast(I32), 0x7F800000, None,
                                            ALU.bitwise_and).then_inc(scale_step, 1)
                    dve.wait_ge(scale_step, 1)
                    nc.vector.tensor_scalar(pow2[:, :], pow2[:, :], 2.0 ** -60, None, ALU.max).then_inc(scale_step, 1)
                    dve.wait_ge(scale_step, 2)
                    nc.vector.reciprocal(inv2[:, :], pow2[:, :]).then_inc(scale_step, 1)
                    dve.wait_ge(scale_step, 3)
                    nc.vector.tensor_copy(inv24[:, :].rearrange("p (t m) -> p t m", m=NM),
                                          inv2[:, :, None].to_broadcast([P, 3, NM])).then_inc(scale_step, 1)
                    nc.vector.tensor_scalar(wfac[:, :], inv2[:, 0:1], 0.125, None, ALU.mult).then_inc(scale_step, 1)
                    nc.vector.tensor_scalar(yfac[:, :], pow2[:, 0:1], pow2[:, 1:2], pow2[:, 2:3],
                                            ALU.mult, ALU.mult).then_inc(scale_step, 1)
                    dve.wait_ge(scale_step, 6)
                    nc.vector.tensor_scalar(yfac[:, :], yfac[:, :], 8.0, tanhg[:, 1:2], ALU.mult, ALU.mult
                                            ).then_inc(scale_step, 1)
                    dve.wait_ge(scale_step, 7)
                    with nc.vector.Fori(SPLIT + 2, LOOP[1] - 1, 2) as n:
                        step(n, 0)
                        step(n + 1, 1)
                    for n in range(LOOP[1], LAST):
                        step(n, n)
                    base = NT + STATS + RSTD + NT
                    dve.wait_ge(stat_step, base)
                    finish_stats(dve, base)
                    finish_rstd(dve, base + STATS, 2)

                @block.gpsimd
                def _(pool):
                    fill = nc.gpsimd.to_reg(MASKED)

                    def mask(j, b):
                        pool.wait_ge(s_copied, j + 1)
                        pool.sem_inc(mask_turn, 1)
                        for half in range(2):
                            v = sc[b][64 * half:64 * half + 64, :, :]
                            nc.gpsimd.affine_select(out=v, in_=v, compare_op=ALU.is_ge, fill=fill, base=0,
                                                    pattern=[[0, HEADS], [-1, S]], channel_multiplier=1
                                                    ).then_inc(masked, 1)

                    def scale(k):
                        src = wall32[:, bass.ds((k + 1) * SLOT, SLOT)]
                        nc.gpsimd.tensor_tensor(src, src, inv24[:, bass.ds(k, 1)].to_broadcast([P, SLOT]), ALU.mult
                                                ).then_inc(scaled, 1)

                    def lo(k, expand):
                        pool.wait_ge(hi_split, k + 1)
                        for s, h, l in zip(*piece(k, expand)):
                            last = nc.gpsimd.tensor_tensor(l, s, h, ALU.subtract)
                        last.then_inc(lo_split, 1)

                    def turn(k, b, expand, lo_expand=None):
                        if has(k + HI_AT - 1):
                            mask(k + HI_AT - 1, b)
                            pool.wait_ge(masked, 2 * (k + HI_AT))
                        if not isinstance(k, int) or k > 0:
                            lo(k - 1, expand if lo_expand is None else lo_expand)
                        if not isinstance(k, int) or k < 3 * NM:
                            scale(k)
                            pool.wait_ge(scaled, k + 1)
                        wait(pool, lo_split, k)

                    BEFORE = HI_AT - 1
                    with nc.gpsimd.Fori(0, BEFORE - 2, 2) as j:
                        mask(j, 0)
                        mask(j + 1, 1)
                    mask(BEFORE - 1, 0)
                    pool.wait_ge(masked, 2 * BEFORE)
                    pool.wait_ge(wmax_done, 3)
                    nc.gpsimd.partition_all_reduce(wmax_all[:, :], wmax[:, :], P, RMAX).then_inc(wmax_shared, 1)
                    pool.wait_ge(wmax_shared, 1)
                    pool.wait_ge(scale_step, 4)
                    turn(0, 1, True)
                    turn(1, 0, True)
                    with nc.gpsimd.Fori(2, 2 * NM - 1, 2) as k:
                        turn(k, 1, True)
                        turn(k + 1, 0, True)
                    for k in range(2 * NM, 3 * NM + 1):
                        turn(k, (k + 1) % 2, False, k == 2 * NM)

        late = ExitStack()
        with late:
            xh = sbuf(late, "xh", [P, KT, T], F16)
            xl = sbuf(late, "xl", [P, KT, T], F16)
            wT = sbuf(late, "wT", [3 * E, T], BF16)
            cum_run = [sbuf(late, f"cum_run{i}", [P, E], BF16) for i in range(2)]
            with ExitStack() as phase:
                NR = AHEAD
                xn2 = [sbuf(phase, f"xn2_{i}", [P, D], F32) for i in range(2)]
                xTf = [sbuf(phase, f"xTf{i}", [P, KT, P], F32) for i in range(2)]
                lg = sbuf(phase, "lg", [P, NR, E], F32)
                lr = sbuf(phase, "lr", [P, NR, E], F32)
                ex = sbuf(phase, "ex", [P, NR, E], F32)
                mk = sbuf(phase, "mk", [P, NR, E], BF16)
                cum = sbuf(phase, "cum", [P, NR, E], BF16)
                w3 = sbuf(phase, "w3", [P, NR, 3, E], BF16)
                top = sbuf(phase, "top", [P, NR, TOP_K], F32)
                lmax = sbuf(phase, "lmax", [P, NR], F32)
                den = sbuf(phase, "den", [P, NR], F32)
                x_ps = [psum(phase, f"x_ps{i}", [P, 512], F32) for i in range(2)]
                lg_ps = psum(phase, "lg_ps", [P, NR, E], F32)
                pos_ps = psum(phase, "pos_ps", [P, NR, E], F32)
                wT_ps = psum(phase, "wT_ps", [P, 8 * P], BF16)

                n2_done, t2_done, f_done, hi_done, lo_done, lg_done = (sem(n) for n in (
                    "n2_done", "t2_done", "f_done", "hi_done", "lo_done", "lg_done"))
                r_step, e_done, cum_done, pos_done, w3_done, wt_done, wt_copied = (sem(n) for n in (
                    "r_step", "e_done", "cum_done", "pos_done", "w3_done", "wt_done", "wt_copied"))

                with nc.Block() as block:
                    @block.vector
                    def _(dve):
                        def norm(t, b):
                            wait(dve, t2_done, t - 1)
                            nc.vector.tensor_scalar(xn2[b][:, :], xs[:, bass.ds(t, 1), :], mean[:, bass.ds(t, 1)],
                                                    rstd[:, bass.ds(t, 1)], ALU.subtract, ALU.mult
                                                    ).then_inc(n2_done, 1)

                        def lo(t, b):
                            wait(dve, hi_done, t + 1)
                            at = bass.ds(t * P, P)
                            nc.vector.tensor_tensor(xl[:, :, at], x_ps[b][:, 0:KT * P].rearrange("p (c n) -> p c n", c=KT),
                                                    xh[:, :, at], ALU.subtract).then_inc(lo_done, 1)

                        norm(0, 0)
                        norm(1, 1)
                        for t in range(NR):
                            lo(t, t % 2)
                            if t + 2 < NR:
                                norm(t + 2, t % 2)

                        count = [0]

                        def step(instruction):
                            count[0] += 1
                            instruction.then_inc(r_step, 1)
                            dve.wait_ge(r_step, count[0])

                        def over_e(v):
                            return v[:, :, None].to_broadcast([P, NR, E])

                        dve.wait_ge(lg_done, NR)
                        step(nc.vector.tensor_reduce(lmax[:, :], lg_ps[:, :, :], AX.X, ALU.max))
                        step(nc.vector.tensor_tensor(lg[:, :, :], lg_ps[:, :, :], over_e(lmax), ALU.subtract))
                        step(nc.vector.tensor_scalar(lg[:, :, :], lg[:, :, :], EXP_FLOOR, None, ALU.max))
                        for t in range(NR):
                            last = nc.vector.max(top[:, t, :], lg[:, t, :])
                        step(last)
                        for t in range(NR):
                            last = nc.vector.match_replace(lr[:, t, :], top[:, t, :], lg[:, t, :], -1e30)
                        step(last)
                        step(nc.vector.tensor_tensor(mk[:, :, :], lr[:, :, :], lg[:, :, :], ALU.not_equal))
                        dve.wait_ge(e_done, 1)
                        step(nc.vector.tensor_tensor(ex[:, :, :], ex[:, :, :], mk[:, :, :], ALU.mult))
                        step(nc.vector.tensor_reduce(den[:, :], ex[:, :, :], AX.X, ALU.add))
                        step(nc.vector.reciprocal(den[:, :], den[:, :]))
                        step(nc.vector.tensor_tensor(ex[:, :, :], ex[:, :, :], over_e(den), ALU.mult))
                        dve.wait_ge(pos_done, 1)
                        step(nc.vector.scalar_tensor_tensor(ex[:, :, :], pos_ps[:, :, :], float(CAP), ex[:, :, :],
                                                            ALU.is_lt, ALU.mult))
                        step(nc.vector.tensor_scalar(ex[:, :, :], ex[:, :, :], wfac[:, 0:1], None, ALU.mult))
                        for part in range(3):
                            step(nc.vector.tensor_copy(w3[:, :, part, :], ex[:, :, :]))
                            if part < 2:
                                step(nc.vector.tensor_tensor(ex[:, :, :], ex[:, :, :], w3[:, :, part, :],
                                                             ALU.subtract))
                        nc.vector.engine_nop().then_inc(w3_done, 1)
                        dve.wait_ge(cum_done, NR)
                        nc.vector.tensor_tensor(cum_run[0][:, :], cum[:, NR - 1, :], mk[:, NR - 1, :], ALU.add
                                                ).then_inc(cum_done, 1)
                        dve.wait_ge(wt_done, 1)
                        nc.vector.tensor_copy(wT[:, 0:NR * P], wT_ps[0:3 * E, 0:NR * P]).then_inc(wt_copied, 1)
                        dve.wait_ge(wt_copied, 1)
                        dve.wait_ge(cum_done, NR + 1)

                    @block.tensor
                    def _(pe):
                        def transpose(t, b):
                            wait(pe, n2_done, t + 1)
                            wait(pe, f_done, t - 1)
                            wait(pe, lo_done, t - 1)
                            for c in range(KT):
                                last = nc.tensor.transpose(x_ps[b][:, c * P:(c + 1) * P],
                                                           xn2[b][:, c * P:(c + 1) * P], identf[:, :])
                            last.then_inc(t2_done, 1)

                        def gate(t, b):
                            wait(pe, f_done, t + 1)
                            for c in range(KT):
                                last = nc.tensor.matmul(lg_ps[:, bass.ds(t, 1), :], xTf[b][:, c, :], gatew[:, c, :],
                                                        start=(c == 0), stop=(c == KT - 1))
                            last.then_inc(lg_done, 1)

                        transpose(0, 0)
                        for t in range(NR):
                            if t + 1 < NR:
                                transpose(t + 1, (t + 1) % 2)
                            gate(t, t % 2)
                        pe.wait_ge(r_step, 6)
                        pe.wait_ge(cum_done, NR)
                        nc.tensor.matmul(pos_ps[:, :, :], tri[:, :], mk[:, :, :], start=True, stop=False)
                        nc.tensor.matmul(pos_ps[:, :, :], onesb[:, :], cum[:, :, :], start=False, stop=True
                                         ).then_inc(pos_done, 1)
                        pe.wait_ge(w3_done, 1)
                        for t in range(NR):
                            last = nc.tensor.transpose(wT_ps[0:3 * E, t * P:(t + 1) * P],
                                                       w3[:, t, :, :].rearrange("p a e -> p (a e)"), identb[:, :])
                        last.then_inc(wt_done, 1)

                    @block.scalar
                    def _(act):
                        def copies(t, b):
                            wait(act, t2_done, t + 1)
                            wait(act, lg_done, t - 1)
                            src = x_ps[b][:, 0:KT * P].rearrange("p (c n) -> p c n", c=KT)
                            nc.scalar.activation(xTf[b][:, :, :], src, ACT.Copy).then_inc(f_done, 1)
                            nc.scalar.activation(xh[:, :, bass.ds(t * P, P)], src, ACT.Copy).then_inc(hi_done, 1)
                        for t in range(NR):
                            copies(t, t % 2)
                        act.wait_ge(r_step, 3)
                        nc.scalar.activation(ex[:, :, :], lg[:, :, :], ACT.Exp).then_inc(e_done, 1)

                    @block.gpsimd
                    def _(pool):
                        nc.gpsimd.memset(cum[:, 0, :], 0.0).then_inc(cum_done, 1)
                        pool.wait_ge(r_step, 6)
                        for t in range(1, NR):
                            pool.wait_ge(cum_done, t)
                            nc.gpsimd.tensor_tensor(cum[:, t, :], cum[:, t - 1, :], mk[:, t - 1, :], ALU.add
                                                    ).then_inc(cum_done, 1)

            with ExitStack() as phase:
                NS = (T // NB) * (NM // 2)
                SPB = NM // 2
                CH = 2 * NI
                assert NS == NT and SPB == TPB
                ysum = sbuf(phase, "ysum", [P, KT, T], F32)
                sg = [sbuf(phase, f"sg{i}", [P, NB], F32) for i in range(2)]
                wb = [sbuf(phase, f"wb{i}", [P, NB], F32) for i in range(2)]
                hf = [sbuf(phase, f"hf{i}", [P, NB], F32) for i in range(2)]
                hh = [sbuf(phase, f"hh{i}", [P, NB], F16) for i in range(NI)]
                hl = [sbuf(phase, f"hl{i}", [P, NB], F16) for i in range(NI)]
                yt = sbuf(phase, "yt", [P, KT, P], F32)
                xn2 = sbuf(phase, "xn2b", [P, D], F32)
                xTf = sbuf(phase, "xTfb", [P, KT, P], F32)
                lg = sbuf(phase, "lgb", [P, E], F32)
                lr = sbuf(phase, "lrb", [P, E], F32)
                ex = sbuf(phase, "exb", [P, E], F32)
                mk = sbuf(phase, "mkb", [P, E], BF16)
                w3 = sbuf(phase, "w3b", [P, 3, E], BF16)
                top = sbuf(phase, "topb", [P, TOP_K], F32)
                lmax = sbuf(phase, "lmaxb", [P, 1], F32)
                den = sbuf(phase, "denb", [P, 1], F32)
                g_ps = [psum(phase, f"g_ps{i}", [P, NB], F32) for i in range(2)]
                u_ps = [psum(phase, f"u_ps{i}", [P, NB], F32) for i in range(2)]
                b_ps = psum(phase, "b_ps", [P, NB], F32)
                y_ps = psum(phase, "y_ps", [P, KT, NB], F32)
                r_ps = psum(phase, "r_ps", [P, 512], F32)
                turned = r_ps[:, 0:KT * P]
                lg_ps = r_ps[:, KT * P:KT * P + E]
                pos_ps = r_ps[:, KT * P + E:KT * P + 2 * E]
                wT_ps = r_ps[:, KT * P + 2 * E:KT * P + 2 * E + P // 2].bitcast(BF16)[0:3 * E, :]

                gu_done, silu_done, wb_made, wb_copied, sgw_done = (sem(n) for n in (
                    "gu_done", "silu_done", "wb_made", "wb_copied", "sgw_done"))
                h_done, hh_done, hl_done, down_done, y_added = (sem(n) for n in (
                    "h_done", "hh_done", "hl_done", "down_done", "y_added"))
                yt_done, ft_done, fin_done, stored = sem("yt_done"), sem("ft_done"), sem("fin_done"), sem("stored")
                rn_done, rt_done, rf_done, rhi_done, rlo_done, rlg_done = (sem(n) for n in (
                    "rn_done", "rt_done", "rf_done", "rhi_done", "rlo_done", "rlg_done"))
                rexp_done, rpos_done, rwt_done, rwt_copied = (sem(n) for n in (
                    "rexp_done", "rpos_done", "rwt_done", "rwt_copied"))
                chain_a, chain_b, carried = sem("chain_a"), sem("chain_b"), sem("carried")
                A_STEPS, B_STEPS = 5, 12

                def over_steps(engine, step):
                    step(0, True, False)
                    with engine.Fori(1, AHEAD) as s:
                        step(s, True, False)
                    step(AHEAD, True, True)
                    with engine.Fori(AHEAD + 1, NT - AHEAD) as s:
                        step(s, True, True)
                    with engine.Fori(NT - AHEAD, NS - 1) as s:
                        step(s, False, True)
                    step(NS - 1, False, True)

                def block_of(s):
                    return s // SPB if isinstance(s, int) else nc.s_assert_within(
                        s >> 2, 0, T // NB - 1, skip_runtime_bounds_check_because="the loop ends at NS")

                def pair_of(s):
                    return s % SPB if isinstance(s, int) else nc.s_assert_within(
                        s & 3, 0, SPB - 1, skip_runtime_bounds_check_because="the loop ends at NS")

                with nc.Block() as block:
                    @block.tensor
                    def _(pe):
                        def spread(s, a, routed=0):
                            m = 2 * s + a
                            wait(pe, wb_copied, m)
                            wait(pe, rwt_copied, routed)
                            nc.tensor.matmul(b_ps[:, :], sel[:, bass.ds(2 * pair_of(s) + a, 1), :],
                                             wT[:, bass.ds(block_of(s) * NB, NB)], start=True, stop=True
                                             ).then_inc(wb_made, 1)

                        def gate_up(s, j):
                            c = CH * s + j
                            wait(pe, silu_done, c - 1)
                            wait(pe, h_done, c - 1)
                            tok = block_of(s) * NB
                            for n, dst in ((0, g_ps), (1, u_ps)):
                                base = (pair_of(s) * 2 + (n * NM + j // NI)) * (2 * SLOT) + (j % NI) * P
                                terms = [(part, xp, half) for half in range(KT) for part, xp in
                                         ((0, xh), (0, xl), (1, xh))]
                                for i, (part, xp, half) in enumerate(terms):
                                    last = nc.tensor.matmul(
                                        dst[j % 2][:, :], wall[:, bass.ds(base + part * SLOT + half * NI * P, P)],
                                        xp[:, half, bass.ds(tok, NB)], start=(i == 0), stop=(i == len(terms) - 1))
                            last.then_inc(gu_done, 1)

                        def down(s, j):
                            c = CH * s + j
                            wait(pe, hl_done, c + 1)
                            if j == 0:
                                wait(pe, y_added, s + 1)
                            base = (pair_of(s) * 2 + (2 * NM + j // NI)) * (2 * SLOT) + (j % NI) * D
                            for half in range(KT):
                                for i, (part, hp) in enumerate(((0, hh), (0, hl), (1, hh))):
                                    last = nc.tensor.matmul(
                                        y_ps[:, half, :], wall[:, bass.ds(base + part * SLOT + half * P, P)],
                                        hp[j % NI][:, :], start=(j == 0 and i == 0), stop=(j == CH - 1 and i == 2))
                            last.then_inc(down_done, 1)

                        def turn_result(f, route):
                            wait(pe, yt_done, f + 1)
                            wait(pe, rwt_copied, f + AHEAD + 1 if route else NT - AHEAD)
                            wait(pe, fin_done, f)
                            for c in range(KT):
                                last = nc.tensor.transpose(turned[:, c * P:(c + 1) * P], yt[:, c, :], identf[:, :])
                            last.then_inc(ft_done, 1)

                        def route_x(s, result):
                            wait(pe, rn_done, s + 1)
                            wait(pe, rwt_copied, s)
                            if result:
                                wait(pe, fin_done, s - AHEAD)
                            for c in range(KT):
                                last = nc.tensor.transpose(turned[:, c * P:(c + 1) * P], xn2[:, c * P:(c + 1) * P],
                                                           identf[:, :])
                            last.then_inc(rt_done, 1)

                        def route_gate(s):
                            wait(pe, rf_done, s + 1)
                            wait(pe, rlo_done, s + 1)
                            for c in range(KT):
                                last = nc.tensor.matmul(lg_ps, xTf[:, c, :], gatew[:, c, :],
                                                        start=(c == 0), stop=(c == KT - 1))
                            last.then_inc(rlg_done, 1)

                        def route_places(s):
                            wait(pe, chain_a, A_STEPS * (s + 1))
                            nc.tensor.matmul(pos_ps, tri[:, :], mk[:, :], start=True, stop=False)
                            nc.tensor.matmul(pos_ps, onesb[:, :], cum_run[0][:, :], start=False, stop=True
                                             ).then_inc(rpos_done, 1)

                        def route_weights(s):
                            wait(pe, chain_b, B_STEPS * (s + 1))
                            nc.tensor.transpose(wT_ps, w3[:, :, :].rearrange("p a e -> p (a e)"), identb[:, :]
                                                ).then_inc(rwt_done, 1)

                        def step(s, route, result, more=True):
                            gate_up(s, 2)
                            down(s, 0)
                            spread(s, 1)
                            if route:
                                route_x(s, result)
                            gate_up(s, 3)
                            down(s, 1)
                            if route:
                                route_gate(s)
                            gate_up(s, 4)
                            down(s, 2)
                            if route:
                                route_places(s)
                            gate_up(s, 5)
                            down(s, 3)
                            if more:
                                spread(s + 1, 0, s if route else NT - AHEAD)
                                gate_up(s + 1, 0)
                            if route:
                                route_weights(s)
                            down(s, 4)
                            if result:
                                turn_result(s - AHEAD, route)
                            if more:
                                gate_up(s + 1, 1)
                            down(s, 5)

                        spread(0, 0)
                        gate_up(0, 0)
                        gate_up(0, 1)
                        over_steps(nc.tensor, lambda s, route, result: step(s, route, result, not isinstance(s, int) or s + 1 < NS))
                        for f in range(NT - AHEAD, NT):
                            turn_result(f, False)

                    @block.scalar
                    def _(act):
                        def copy_wb(s, a):
                            wait(act, wb_made, 2 * s + a + 1)
                            wait(act, sgw_done, CH * (s - 1) + NI * (a + 1))
                            nc.scalar.activation(wb[a][:, :], b_ps[:, :], ACT.Copy).then_inc(wb_copied, 1)

                        def silu(s, j):
                            c = CH * s + j
                            wait(act, gu_done, c + 1)
                            wait(act, h_done, c - 1)
                            nc.scalar.activation(sg[j % 2][:, :], g_ps[j % 2][:, :], ACT.Silu, scale=pow2[:, 0:1]
                                                 ).then_inc(silu_done, 1)

                        def hi(s, j):
                            c = CH * s + j
                            wait(act, h_done, c + 1)
                            wait(act, down_done, c - 2)
                            nc.scalar.activation(hh[j % NI][:, :], hf[j % 2][:, :], ACT.Copy).then_inc(hh_done, 1)

                        def take_sum(f):
                            wait(act, y_added, min(f + AHEAD, NS + 1) if isinstance(f, int) else f + AHEAD)
                            wait(act, ft_done, f)
                            nc.scalar.activation(yt[:, :, :], ysum[:, :, bass.ds(f * P, P)], ACT.Copy
                                                 ).then_inc(yt_done, 1)

                        def step(s, route, result):
                            for j in range(CH):
                                if j == NI:
                                    copy_wb(s, 1)
                                silu(s, j)
                                if j == 4 and route:
                                    wait(act, chain_a, A_STEPS * s + 2)
                                    wait(act, chain_b, B_STEPS * s)
                                    nc.scalar.activation(ex[:, :], lg[:, :], ACT.Exp).then_inc(rexp_done, 1)
                                hi(s, j)
                                if j == 2 and route:
                                    wait(act, rt_done, s + 1)
                                    wait(act, rlg_done, s)
                                    src = turned.rearrange("p (c n) -> p c n", c=KT)
                                    nc.scalar.activation(xTf[:, :, :], src, ACT.Copy).then_inc(rf_done, 1)
                                    nc.scalar.activation(xh[:, :, bass.ds((s + AHEAD) * P, P)], src, ACT.Copy
                                                         ).then_inc(rhi_done, 1)
                                if j == 3 and result:
                                    take_sum(s - AHEAD)
                            if not isinstance(s, int) or s + 1 < NS:
                                copy_wb(s + 1, 0)

                        copy_wb(0, 0)
                        over_steps(nc.scalar, step)
                        for f in range(NT - AHEAD, NT):
                            take_sum(f)

                    @block.gpsimd
                    def _(pool):
                        nc.gpsimd.memset(ysum[:, :, :], 0.0).then_inc(y_added, 1)

                        with nc.gpsimd.Fori(0, NS) as s:
                            for j in range(CH):
                                c = CH * s + j
                                pool.wait_ge(silu_done, c + 1)
                                if j % NI == 0:
                                    pool.wait_ge(wb_copied, 2 * s + j // NI + 1)
                                nc.gpsimd.tensor_tensor(sg[j % 2][:, :], sg[j % 2][:, :], wb[j // NI][:, :], ALU.mult
                                                        ).then_inc(sgw_done, 1)

                    @block.vector
                    def _(dve):
                        def hidden(s, j):
                            c = CH * s + j
                            wait(dve, sgw_done, c + 1)
                            wait(dve, hl_done, c - 1)
                            nc.vector.tensor_tensor(hf[j % 2][:, :], sg[j % 2][:, :], u_ps[j % 2][:, :], ALU.mult
                                                    ).then_inc(h_done, 1)

                        def lo(s, j):
                            c = CH * s + j
                            wait(dve, hh_done, c + 1)
                            wait(dve, down_done, c - 2)
                            nc.vector.tensor_tensor(hl[j % NI][:, :], hf[j % 2][:, :], hh[j % NI][:, :], ALU.subtract
                                                    ).then_inc(hl_done, 1)

                        def add(s):
                            wait(dve, down_done, CH * (s + 1))
                            wait(dve, y_added, s + 1)
                            v = ysum[:, :, bass.ds(block_of(s) * NB, NB)]
                            nc.vector.tensor_tensor(v, v, y_ps[:, :, :], ALU.add).then_inc(y_added, 1)

                        def result_row(f):
                            wait(dve, ft_done, f + 1)
                            row = xs[:, bass.ds(f, 1), :]
                            nc.vector.scalar_tensor_tensor(row, turned[:, None, :], yfac[:, 0:1], row,
                                                           ALU.mult, ALU.add).then_inc(fin_done, 1)

                        def norm(s):
                            wait(dve, rt_done, s)
                            t = s + AHEAD
                            nc.vector.tensor_scalar(xn2[:, :], xs[:, bass.ds(t, 1), :], mean[:, bass.ds(t, 1)],
                                                    rstd[:, bass.ds(t, 1)], ALU.subtract, ALU.mult
                                                    ).then_inc(rn_done, 1)

                        def route_lo(s):
                            wait(dve, rhi_done, s + 1)
                            at = bass.ds((s + AHEAD) * P, P)
                            nc.vector.tensor_tensor(xl[:, :, at], turned.rearrange("p (c n) -> p c n", c=KT),
                                                    xh[:, :, at], ALU.subtract).then_inc(rlo_done, 1)

                        def chained(signal, steps, s):
                            count = [0]

                            def link(instruction):
                                count[0] += 1
                                instruction.then_inc(signal, 1)
                                wait(dve, signal, steps * s + count[0])
                            return link

                        def pick(s):
                            link = chained(chain_a, A_STEPS, s)
                            wait(dve, rlg_done, s + 1)
                            wait(dve, rexp_done, s)
                            link(nc.vector.tensor_reduce(lmax[:, :], lg_ps, AX.X, ALU.max))
                            link(nc.vector.tensor_scalar(lg[:, :], lg_ps, lmax[:, 0:1], EXP_FLOOR,
                                                         ALU.subtract, ALU.max))
                            dve.sem_inc(carried, 1)
                            link(nc.vector.max(top[:, :], lg[:, :]))
                            dve.sem_inc(carried, 1)
                            link(nc.vector.match_replace(lr[:, :], top[:, :], lg[:, :], -1e30))
                            wait(dve, rpos_done, s)
                            link(nc.vector.tensor_tensor(mk[:, :], lr[:, :], lg[:, :], ALU.not_equal))

                        def weigh(s):
                            link = chained(chain_b, B_STEPS, s)
                            wait(dve, rexp_done, s + 1)
                            link(nc.vector.tensor_tensor(ex[:, :], ex[:, :], mk[:, :], ALU.mult))
                            link(nc.vector.tensor_reduce(den[:, :], ex[:, :], AX.X, ALU.add))
                            link(nc.vector.reciprocal(den[:, :], den[:, :]))
                            link(nc.vector.tensor_scalar(ex[:, :], ex[:, :], den[:, 0:1], None, ALU.mult))
                            wait(dve, rpos_done, s + 1)
                            link(nc.vector.scalar_tensor_tensor(ex[:, :], pos_ps, float(CAP), ex[:, :],
                                                                ALU.is_lt, ALU.mult))
                            link(nc.vector.tensor_scalar(ex[:, :], ex[:, :], wfac[:, 0:1], None, ALU.mult))
                            wait(dve, rwt_done, s)
                            for part in range(3):
                                link(nc.vector.tensor_copy(w3[:, part, :], ex[:, :]))
                                if part < 2:
                                    link(nc.vector.tensor_tensor(ex[:, :], ex[:, :], w3[:, part, :], ALU.subtract))
                            link(nc.vector.tensor_tensor(cum_run[0][:, :], cum_run[0][:, :], mk[:, :], ALU.add))

                        def copy_weights(s):
                            wait(dve, rwt_done, s + 1)
                            nc.vector.tensor_copy(wT[:, bass.ds((s + AHEAD) * P, P)], wT_ps).then_inc(rwt_copied, 1)

                        def step(s, route, result):
                            hidden(s, 0)
                            if route:
                                norm(s)
                            lo(s, 0)
                            if not isinstance(s, int) or s > 0:
                                add(s - 1)
                            hidden(s, 1)
                            lo(s, 1)
                            hidden(s, 2)
                            lo(s, 2)
                            if route:
                                route_lo(s)
                            hidden(s, 3)
                            if route:
                                pick(s)
                            lo(s, 3)
                            hidden(s, 4)
                            if route:
                                weigh(s)
                            lo(s, 4)
                            hidden(s, 5)
                            lo(s, 5)
                            if route:
                                copy_weights(s)
                            if result:
                                result_row(s - AHEAD)

                        over_steps(nc.vector, step)
                        add(NS - 1)
                        for f in range(NT - AHEAD, NT):
                            result_row(f)

                    @block.sync
                    def _(sp):
                        with nc.sync.Fori(0, NT) as f:
                            sp.wait_ge(fin_done, f + 1)
                            sp.dma_start(out_rows[bass.ds(f * P, P), :], xs[:, bass.ds(f, 1), :]).then_inc(stored, 16)
                        sp.wait_ge(stored, 16 * NT)


_INS = ['x', 'ctx_2048', 'g_xattn', 'g_ffn', 'L0_ffn_gate_w', 'L0_ffn_w_gate', 'L0_ffn_w_up', 'L0_ffn_w_down']


def kernel(**inputs):
    import numpy as _np
    import concourse.bacc as _bacc
    from concourse import mybir as _mybir
    from concourse.bass_utils import run_bass_kernel_spmd as _run

    nc = _bacc.Bacc("TRN2", target_bir_lowering=False, num_devices=1)
    arrays, args = {}, []
    for name in _INS:
        a = _np.ascontiguousarray(inputs[name])
        arrays[f"in_{name}_dram"] = a
        args.append(nc.dram_tensor(f"in_{name}_dram", a.shape, _mybir.dt.from_np(a.dtype), kind="ExternalInput").ap())
    args.append(nc.dram_tensor("out_0_dram", arrays["in_x_dram"].shape, _mybir.dt.float32, kind="ExternalOutput").ap())
    build(nc, *args)
    r = _run(nc, [arrays], core_ids=[0])
    return r.results[0]["out_0_dram"]
```

```python
from contextlib import ExitStack

import concourse.bass as bass
from concourse import mybir

P = 128
F32 = mybir.dt.float32
F16 = mybir.dt.float16
BF16 = mybir.dt.bfloat16
I32 = mybir.dt.int32
ALU = mybir.AluOpType
ACT = mybir.ActivationFunctionType
AX = mybir.AxisListType
RMAX = bass.bass_isa.ReduceOp.max

HEADS = 16
TOP_K = 8
EPS = 1e-5
MASKED = -10000.0
EXP_FLOOR = -104.0


def build(nc, x, ctx_in, g_xattn, g_ffn, gate_w, w_gate, w_up, w_down, out):
    B, S, D = x.shape
    E, _, INTER = w_gate.shape
    T = B * S
    NT = T // P
    HD = D // HEADS
    KT = D // P
    CAP = 2 * (T * TOP_K // E)
    G4 = P // 32
    NM = E // G4
    NI = INTER // 32
    NB = 512
    TPB = NB // P
    AHEAD = 5
    NA = AHEAD + 2
    RING = 4 * TPB
    SLOT = NI * P * KT
    assert S == 64 and HD == 16 and KT == 2 and SLOT == NI * D

    x_rows = x.rearrange("b s d -> (b s) d")
    ctx_rows = ctx_in.rearrange("b s d -> (b s) d")
    out_rows = out.rearrange("b s d -> (b s) d")

    persist = ExitStack()

    def sbuf(stack, name, shape, dt):
        return stack.enter_context(nc.sbuf_tensor(name, shape, dt))

    def psum(stack, name, shape, dt):
        return stack.enter_context(nc.psum_tensor(name, shape, dt))

    def sem(name):
        return persist.enter_context(nc.semaphore(name))

    with persist:
        xs = sbuf(persist, "xs", [P, NT, D], F32)
        wall = sbuf(persist, "wall", [P, 3 * (NM + 1) * SLOT * 2], F16)
        wall32 = wall[:, :].bitcast(F32)
        gatew = sbuf(persist, "gatew", [P, KT, E], F32)
        identf = sbuf(persist, "identf", [P, P], F32)
        identb = sbuf(persist, "identb", [P, P], BF16)
        tri = sbuf(persist, "tri", [P, P], BF16)
        onesb = sbuf(persist, "onesb", [P, P], BF16)
        sel = sbuf(persist, "sel", [3 * E, NM, P], BF16)
        parity = sbuf(persist, "parity", [P, 2], F32)
        gates = sbuf(persist, "gates", [P, 2], F32)
        spare_g = sbuf(persist, "spare_g", [P, 2], F32)
        tanhg = sbuf(persist, "tanhg", [P, 2], F32)
        stats = sbuf(persist, "stats", [P, NT, 6], F32)
        mean = sbuf(persist, "mean", [P, NT], F32)
        rstd = sbuf(persist, "rstd", [P, NT], F32)
        va_all = sbuf(persist, "va", [P, NT], F32)
        vb_all = sbuf(persist, "vb", [P, NT], F32)
        mean2 = sbuf(persist, "mean2", [P, AHEAD], F32)
        rstd2 = sbuf(persist, "rstd2", [P, AHEAD], F32)
        wmax = sbuf(persist, "wmax", [P, 3], F32)
        wmax24 = sbuf(persist, "wmax24", [P, 3 * NM], F32)
        wmax_all = sbuf(persist, "wmax_all", [P, 3], F32)
        pow2 = sbuf(persist, "pow2", [P, 3], F32)
        inv2 = sbuf(persist, "inv2", [P, 3], F32)
        wfac = sbuf(persist, "wfac", [P, 1], F32)
        yfac = sbuf(persist, "yfac", [P, 1], F32)

        x_in = [sem(f"x_in{i}") for i in range(4)]
        small_in = sem("small_in")
        w_in = [sem(f"w_in{i}") for i in range(3)]
        zeros_set, masks_set = sem("zeros_set"), sem("masks_set")
        tanh_done = sem("tanh_done")
        stat_step = sem("stat_step")
        second_step = sem("second_step")
        rest_step = sem("rest_step")
        sqrt_done = sem("sqrt_done")
        wmax_step, wmax_done, wmax_shared, scale_step = sem("wmax_step"), sem("wmax_done"), sem("wmax_shared"), sem("scale_step")

        def finish_stats(dve, signal, base, tiles, mean):
            va, vb = va_all[:, tiles], vb_all[:, tiles]
            me, m2e, mo, m2o = (stats[:, tiles, k] for k in (1, 2, 4, 5))
            count = [base]

            def step(instruction):
                count[0] += 1
                instruction.then_inc(signal, 1)
                dve.wait_ge(signal, count[0])

            step(nc.vector.tensor_tensor(va, me, mo, ALU.subtract))
            step(nc.vector.tensor_tensor(mean, me, mo, ALU.add))
            step(nc.vector.tensor_tensor(vb, m2e, m2o, ALU.add))
            step(nc.vector.tensor_scalar(mean, mean, 0.5, None, ALU.mult))
            step(nc.vector.scalar_tensor_tensor(va, va, 0.25, va, ALU.mult, ALU.mult))
            step(nc.vector.tensor_scalar(vb, vb, 1.0 / D, EPS, ALU.mult, ALU.add))
            step(nc.vector.tensor_tensor(vb, vb, va, ALU.add))
            return count[0]

        def finish_rstd(dve, signal, base, which, tiles, rstd):
            va, vb = va_all[:, tiles], vb_all[:, tiles]
            count = [base]

            def step(instruction):
                count[0] += 1
                instruction.then_inc(signal, 1)
                dve.wait_ge(signal, count[0])

            dve.wait_ge(sqrt_done, which)
            step(nc.vector.reciprocal(rstd, va))
            step(nc.vector.tensor_tensor(va, rstd, rstd, ALU.mult))
            step(nc.vector.tensor_tensor(va, va, vb, ALU.mult))
            step(nc.vector.tensor_scalar(va, va, -0.5, 1.5, ALU.mult, ALU.add))
            step(nc.vector.tensor_tensor(rstd, rstd, va, ALU.mult))
            return count[0]

        EARLY = NT // 4
        STATS = 7
        RSTD = 5

        def load_x(sp, i):
            n = NT // 4
            sp.dma_start(xs[:, i * n:(i + 1) * n, :],
                         x_rows[i * n * P:(i + 1) * n * P, :].rearrange("(t p) d -> p t d", p=P)
                         ).then_inc(x_in[i], 16)

        with nc.Block() as block:
            @block.sync
            def _(sp):
                load_x(sp, 0)
                sp.dma_start(gatew[:, :, :], gate_w.rearrange("(k p) e -> p k e", p=P)).then_inc(small_in, 16)
                for i, g in enumerate((g_xattn, g_ffn)):
                    sp.dma_start(gates[:, i:i + 1], g.rearrange("(a b) -> a b", b=1).to_broadcast([P, 1])
                                 ).then_inc(small_in, 16)

            @block.gpsimd
            def _(pool):
                nc.gpsimd.memset(identf[:, :], 0.0).then_inc(zeros_set, 1)
                nc.gpsimd.memset(identb[:, :], 0.0).then_inc(zeros_set, 1)
                nc.gpsimd.memset(tri[:, :], 1.0).then_inc(zeros_set, 1)
                nc.gpsimd.memset(sel[:, :, :], 0.0).then_inc(zeros_set, 1)
                nc.gpsimd.memset(parity[:, :], 1.0).then_inc(zeros_set, 1)
                nc.gpsimd.memset(onesb[:, :], 1.0).then_inc(zeros_set, 1)
                pool.wait_ge(zeros_set, 6)
                made = [0]

                def mask(v, compare, fill, base, pattern, per_row):
                    nc.gpsimd.affine_select(out=v, in_=v, compare_op=compare, fill=fill, base=base, pattern=pattern,
                                            channel_multiplier=per_row).then_inc(masks_set, 1)
                    made[0] += 1
                    pool.wait_ge(masks_set, made[0])

                for m in (identf, identb):
                    mask(m[:, :], ALU.not_equal, 1.0, 0, [[-1, P]], 1)
                mask(tri[:, :], ALU.is_gt, 0.0, 0, [[1, P]], -1)
                for part in range(3):
                    mask(sel[part * E:(part + 1) * E, :, :].rearrange("p m (q r) -> p m q r", q=G4),
                         ALU.not_equal, 1.0, 0, [[-G4, NM], [-1, G4], [0, 32]], 1)
                for g in range(G4):
                    even, odd = (parity[32 * g:32 * g + 32, h:h + 1] for h in range(2))
                    mask(even, ALU.is_ge, 0.0, HD - 1, [[0, 1]], -1)
                    mask(odd, ALU.is_ge, 0.0, -HD, [[0, 1]], 1)

            @block.vector
            def _(dve):
                dve.wait_ge(x_in[0], 16)
                for t in range(EARLY):
                    nc.vector.bn_stats(stats[:, t, :], xs[:, t, :]).then_inc(stat_step, 1)
                dve.wait_ge(stat_step, EARLY)
                finish_stats(dve, stat_step, EARLY, slice(0, EARLY), mean[:, 0:EARLY])
                finish_rstd(dve, stat_step, EARLY + STATS, 1, slice(0, EARLY), rstd[:, 0:EARLY])

            @block.scalar
            def _(act):
                n = EARLY
                act.wait_ge(stat_step, EARLY + STATS)
                nc.scalar.activation(va_all[:, 0:n], vb_all[:, 0:n], ACT.Sqrt).then_inc(sqrt_done, 1)
                act.wait_ge(small_in, 48)
                nc.scalar.activation(tanhg[:, :], gates[:, :], ACT.Tanh).then_inc(tanh_done, 1)
                act.wait_ge(tanh_done, 1)

        with ExitStack() as phase:
            cnat = [sbuf(phase, f"cnat{i}", [P, D], F32) for i in range(2)]
            cdup = [sbuf(phase, f"cdup{i}", [P, 2, D], F32) for i in range(2)]
            xn = [sbuf(phase, f"xn{i}", [P, D], F32) for i in range(2)]
            qT = [sbuf(phase, f"qT{i}", [P, KT, P], F32) for i in range(2)]
            kpair = [sbuf(phase, f"kpair{i}", [P, KT * 2, 2, S], F32) for i in range(2)]
            sc = [sbuf(phase, f"sc{i}", [P, HEADS, S], F32) for i in range(2)]
            pr = [sbuf(phase, f"pr{i}", [P, HEADS * S], F32) for i in range(2)]
            pT = [sbuf(phase, f"pT{i}", [P, HEADS // 2, P], F32) for i in range(2)]
            vpair = [sbuf(phase, f"vpair{i}", [P, 2, HEADS // 2, 2, HD], F32) for i in range(2)]
            oT = [sbuf(phase, f"oT{i}", [P, KT, P], F32) for i in range(2)]
            smax = sbuf(phase, "smax", [P, HEADS], F32)
            den = [sbuf(phase, f"den{i}", [P, HEADS], F32) for i in range(2)]
            rden = [sbuf(phase, f"rden{i}", [P, HEADS], F32) for i in range(2)]
            att = sbuf(phase, "att", [P, HEADS, HD], F32)
            qk_ps = psum(phase, "qk_ps", [P, 2 * KT, P], F32)
            s_ps = psum(phase, "s_ps", [P, G4, 512], F32)
            pT_ps = psum(phase, "pT_ps", [P, HEADS // 2, P], F32)
            o_ps = psum(phase, "o_ps", [P, 2, KT * P], F32)
            oT_ps = o_ps[:, 0, :].rearrange("p (c n) -> p c n", c=KT)
            cnat_in = [sem(f"cnat_in{i}") for i in range(2)]
            cdup_in = [sem(f"cdup_in{i}") for i in range(2)]
            ln_done, tqk_done, q_done, k_done = sem("ln_done"), sem("tqk_done"), sem("q_done"), sem("k_done")
            s_done, s_copied, masked, max_done, sub_done = (sem(n) for n in (
                "s_done", "s_copied", "masked", "max_done", "sub_done"))
            exp_done, tp_done, pT_done, v_done = (sem(n) for n in (
                "exp_done", "tp_done", "pT_done", "v_done"))
            rden_step, att_done, x1_done, v_init = sem("rden_step"), sem("att_done"), sem("x1_done"), sem("v_init")
            mask_turn, den_done, oT_made, oT_done, o_done = (sem(n) for n in (
                "mask_turn", "den_done", "oT_made", "oT_done", "o_done"))
            scaled, hi_split, lo_split = sem("scaled"), sem("hi_split"), sem("lo_split")

            FIRST, LAST = -4, NA + 4
            SPLIT_AT, SPLIT = NA - 1, 3
            REST_AT = 3
            SECOND_AT = LAST - 2
            LATER = 12

            def pipeline(step):
                for n in range(FIRST, LAST):
                    step(n, n)

            def has(j):
                return 0 <= j < NA

            def wait(engine, s, count):
                if not isinstance(count, int) or count > 0:
                    engine.wait_ge(s, count)

            def piece(i):
                n, k = SLOT, i % 3 * (NM + 1) + i // 3
                src = wall32[:, (k + 1) * n:(k + 2) * n]
                if i % 3 == 2:
                    return [src], *([wall[:, (2 * k + a) * n:(2 * k + a + 1) * n]] for a in range(2))
                src = src.rearrange("p (q c i r) -> p c i q r", q=G4, c=KT, i=NI)
                return [src[:, c] for c in range(KT)], *([wall[:, bass.ds((2 * k + a) * n + c * NI * P, NI * P)]
                                                          .rearrange("p (i q r) -> p i q r", i=NI, q=G4)
                                                          for c in range(KT)] for a in range(2))

            def landed(j, b, per):
                return (j - b) * 8 * per + 16 * per

            in_place = [i for i in range(3 * NM) if i % 3 == 0 or i % 6 == 1]

            def inverse(i):
                return inv2[:, i % 3:i % 3 + 1]

            def scale(pool, i):
                k = i % 3 * (NM + 1) + i // 3 + 1
                src = wall32[:, k * SLOT:(k + 1) * SLOT]
                nc.gpsimd.tensor_tensor(src, src, inverse(i).to_broadcast([P, SLOT]), ALU.mult).then_inc(scaled, 1)

            def hi(act, i):
                wait(act, lo_split, i - 2)
                if i in in_place:
                    act.wait_ge(scaled, in_place.index(i) + 1)
                src, his, _ = piece(i)
                for s, h in zip(src, his):
                    last = nc.scalar.activation(h, s, ACT.Copy, scale=1.0 if i in in_place else inverse(i))
                last.then_inc(hi_split, 1)

            def lo(dve, i):
                dve.wait_ge(hi_split, i + 1)
                for part in zip(*piece(i)):
                    if i in in_place:
                        s, h, l = part
                        last = nc.vector.tensor_tensor(l, s, h, ALU.subtract)
                    else:
                        for s, h, l in [part] if i % 3 == 2 else [[v[:, c] for v in part] for c in range(NI)]:
                            last = nc.vector.scalar_tensor_tensor(l, s, inverse(i), h, ALU.mult, ALU.subtract)
                last.then_inc(lo_split, 1)

            def pieces(i, first, per, end):
                return range(min(first + i * per, end), min(first + (i + 1) * per, end)) if i >= 0 else ()

            with nc.Block() as block:
                @block.sync
                def _(sp):
                    def step(n, k):
                        j, b = n + 4, k % 2
                        if has(j):
                            wait(sp, tqk_done, j - 1)
                            sp.dma_start(cnat[b][:, :], ctx_rows[bass.ds(j * P, P), :]).then_inc(cnat_in[b], 16)
                        j, b = n, k % 2
                        if has(j):
                            wait(sp, v_done, j - 1)
                            src = ctx_rows[bass.ds(j * P, P), :].rearrange("(b s) d -> s b d", b=2)
                            for half in range(2):
                                sp.dma_start(cdup[b][64 * half:64 * half + 64, :, :], src).then_inc(cdup_in[b], 16)

                    def weights(i):
                        if i < 2 * NM:
                            w = (w_gate, w_up)[i // NM][i % NM * G4:i % NM * G4 + G4]
                            at = (i // NM * (NM + 1) + i % NM + 1) * SLOT
                            sp.dma_start(wall32[:, at:at + SLOT].rearrange("p (a i) -> p a i", i=INTER),
                                         w.rearrange("e (k p) i -> p (e k) i", p=P)).then_inc(w_in[i // NM], 16)
                        else:
                            q, i = (i - 2 * NM) // NI, (i - 2 * NM) % NI
                            at = (2 * (NM + 1) + 1) * SLOT
                            sp.dma_start(wall32[32 * q:32 * q + 32, at:at + NM * SLOT].rearrange(
                                "p (m i n) -> p i m n", m=NM, i=NI)[:, i],
                                w_down.rearrange("(m q) (i r) n -> q i r m n", q=G4, r=32)[q, i]).then_inc(w_in[2], 16)

                    for n in range(FIRST, LAST):
                        step(n, n)
                        if n == FIRST + 1:
                            for i in range(1, 4):
                                load_x(sp, i)
                        if -2 <= n < 4:
                            for i in range(5 * (n + 2), min(5 * (n + 3), 2 * NM + G4 * NI)):
                                weights(i)

                @block.tensor
                def _(pe):
                    def step(n, k):
                        j, b = n + 1, (k + 1) % 2
                        if has(j):
                            wait(pe, ln_done, j + 1)
                            wait(pe, cnat_in[b], landed(j, b, 1))
                            wait(pe, q_done, j)
                            for c in range(KT):
                                nc.tensor.transpose(qk_ps[:, c, :], xn[b][:, c * P:(c + 1) * P], identf[:, :])
                            for c in range(KT):
                                last = nc.tensor.transpose(qk_ps[:, KT + c, :], cnat[b][:, c * P:(c + 1) * P],
                                                           identf[:, :])
                            last.then_inc(tqk_done, 1)
                        j, b = n - 2, k % 2
                        if has(j):
                            wait(pe, exp_done, j + 1)
                            wait(pe, pT_done, j)
                            for c in range(HEADS // 2):
                                last = nc.tensor.transpose(pT_ps[:, c, :], pr[b][:, c * P:(c + 1) * P], identf[:, :])
                            last.then_inc(tp_done, 1)
                        j, b = n - 4, k % 2
                        if has(j):
                            wait(pe, oT_done, j + 1)
                            for c in range(KT):
                                last = nc.tensor.transpose(o_ps[:, 1, c * P:(c + 1) * P], oT[b][:, c, :], identf[:, :])
                            last.then_inc(o_done, 1)
                        j, b = n, k % 2
                        if has(j):
                            wait(pe, q_done, j + 1)
                            wait(pe, s_copied, j)
                            for c in range(KT):
                                for h in range(2):
                                    for g in range(G4):
                                        rows = slice(32 * g, 32 * g + 32)
                                        last = nc.tensor.matmul(
                                            s_ps[64 * h:64 * h + 64, g, c * P:(c + 1) * P],
                                            qT[b][rows, c, 64 * h:64 * h + 64],
                                            kpair[b][rows, 2 * c + h, :, :].rearrange("p a s -> p (a s)"),
                                            start=True, stop=True)
                            last.then_inc(s_done, 1)
                        j, b = n - 3, (k + 1) % 2
                        if has(j):
                            wait(pe, pT_done, j + 1)
                            wait(pe, v_done, j + 1)
                            wait(pe, att_done, j)
                            for h in range(2):
                                for pair in range(HEADS // 2):
                                    c, g = pair // G4, pair % G4
                                    last = nc.tensor.matmul(
                                        oT_ps[32 * g:32 * g + 32, c, 64 * h:64 * h + 64],
                                        vpair[b][:, h, pair, :, :].rearrange("p a d -> p (a d)"),
                                        pT[b][:, pair, 64 * h:64 * h + 64], start=True, stop=True)
                            last.then_inc(oT_made, 1)
                    pipeline(step)

                @block.scalar
                def _(act):
                    def step(n, k):
                        if n == SPLIT_AT:
                            act.wait_ge(scale_step, 3)
                        if n == SECOND_AT + 1:
                            act.wait_ge(second_step, STATS)
                            nc.scalar.activation(va_all[:, 0:AHEAD], vb_all[:, 0:AHEAD], ACT.Sqrt).then_inc(sqrt_done, 1)
                        if n == REST_AT + 1:
                            act.wait_ge(rest_step, NT - EARLY + STATS)
                            nc.scalar.activation(va_all[:, EARLY:NT], vb_all[:, EARLY:NT], ACT.Sqrt
                                                 ).then_inc(sqrt_done, 1)
                        j, b = n + 1, (k + 1) % 2
                        if has(j):
                            wait(act, k_done, j + 1)
                            wait(act, s_done, j - 1)
                            nc.scalar.activation(qT[b][:, :, :], qk_ps[:, 0:KT, :], ACT.Copy).then_inc(q_done, 1)
                        j, b = n - 2, k % 2
                        if has(j):
                            wait(act, tp_done, j + 1)
                            wait(act, oT_made, j - 1)
                            nc.scalar.activation(pT[b][:, :, :], pT_ps[:, :, :], ACT.Copy).then_inc(pT_done, 1)
                        j, b = n, k % 2
                        if has(j):
                            wait(act, s_done, j + 1)
                            wait(act, exp_done, j - 1)
                            src = s_ps[:, :, 0:2 * P].rearrange("p g (c n) -> p g c n", c=KT)
                            dst = sc[b][:, :, :].rearrange("p (c g a) s -> p g c (a s)", c=KT, g=G4)
                            nc.scalar.activation(dst, src, ACT.Copy, scale=HD ** -0.5).then_inc(s_copied, 1)
                        j, b = n - 1, (k + 1) % 2
                        if has(j):
                            wait(act, sub_done, j + 1)
                            wait(act, tp_done, j - 1)
                            wait(act, den_done, j - 1)
                            nc.scalar.activation(pr[b][:, :], sc[b][:, :, :].rearrange("p h s -> p (h s)"),
                                                 ACT.Exp).then_inc(exp_done, 1)
                        j, b = n - 3, (k + 1) % 2
                        if has(j):
                            wait(act, oT_made, j + 1)
                            wait(act, o_done, j - 1)
                            nc.scalar.activation(oT[b][:, :, :], oT_ps, ACT.Copy).then_inc(oT_done, 1)
                        for i in pieces(n - SPLIT_AT, 0, SPLIT, LATER):
                            hi(act, i)

                    pipeline(step)

                @block.vector
                def _(dve):
                    def step(n, k):
                        j, b = n + 1, (k + 1) % 2
                        if has(j):
                            wait(dve, tqk_done, j + 1)
                            wait(dve, s_done, j - 1)
                            nc.vector.tensor_tensor(
                                kpair[b][:, :, :, :],
                                qk_ps[:, KT:2 * KT, :].rearrange("p c (h s) -> p (c h) s", h=2)[:, :, None, :]
                                .to_broadcast([P, 2 * KT, 2, S]),
                                parity[:, None, :, None].to_broadcast([P, 2 * KT, 2, S]),
                                ALU.mult).then_inc(k_done, 1)
                        j, b = n + 2, k % 2
                        if has(j):
                            wait(dve, tqk_done, j - 1)
                            nc.vector.tensor_scalar(xn[b][:, :], xs[:, bass.ds(j, 1), :], mean[:, bass.ds(j, 1)],
                                                    rstd[:, bass.ds(j, 1)], ALU.subtract, ALU.mult
                                                    ).then_inc(ln_done, 1)
                        j, b = n - 2, k % 2
                        if has(j):
                            wait(dve, cdup_in[b], landed(j, b, 2))
                            wait(dve, oT_made, j - 1)
                            src = cdup[b][:, :, :].rearrange("p h (c a d) -> p h c a d", a=2, d=HD)
                            for half in range(2):
                                rows = slice(64 * half, 64 * half + 64)
                                last = nc.vector.tensor_copy(vpair[b][rows, :, :, half, 0:HD], src[rows, :, :, half, :])
                            last.then_inc(v_done, 1)
                        j, b = n - 4, k % 2
                        if has(j):
                            wait(dve, o_done, j + 1)
                            wait(dve, x1_done, j)
                            wait(dve, rden_step, 2 * j + 2)
                            nc.vector.tensor_tensor(att[:, :, :], o_ps[:, 1, :].rearrange("p (h d) -> p h d", d=HD),
                                                    rden[b][:, :, None].to_broadcast([P, HEADS, HD]),
                                                    ALU.mult).then_inc(att_done, 1)
                            wait(dve, att_done, j + 1)
                            row = xs[:, bass.ds(j, 1), :]
                            nc.vector.tensor_tensor(row, row, att[:, :, :].rearrange("p h d -> p (h d)")[:, None, :],
                                                    ALU.add).then_inc(x1_done, 1)
                            wait(dve, x1_done, j + 1)
                            nc.vector.bn_stats(stats[:, bass.ds(j, 1), :], row).then_inc(stat_step, 1)
                        j, b = n - 1, (k + 1) % 2
                        if has(j):
                            wait(dve, masked, 2 * j + 2)
                            wait(dve, sub_done, j)
                            nc.vector.tensor_reduce(smax[:, :], sc[b][:, :, :], AX.X, ALU.max).then_inc(max_done, 1)
                            wait(dve, max_done, j + 1)
                            nc.vector.tensor_tensor(sc[b][:, :, :], sc[b][:, :, :],
                                                    smax[:, :, None].to_broadcast([P, HEADS, S]),
                                                    ALU.subtract).then_inc(sub_done, 1)
                        j, b = n - 2, k % 2
                        if has(j):
                            wait(dve, exp_done, j + 1)
                            wait(dve, att_done, j - 1)
                            nc.vector.tensor_reduce(den[b][:, :], pr[b][:, :].rearrange("p (h s) -> p h s", s=S), AX.X,
                                                    ALU.add).then_inc(den_done, 1)
                            wait(dve, den_done, j + 1)
                            nc.vector.reciprocal(rden[b][:, :], den[b][:, :]).then_inc(rden_step, 1)
                            wait(dve, rden_step, 2 * j + 1)
                            nc.vector.tensor_scalar(rden[b][:, :], rden[b][:, :], tanhg[:, 0:1], None, ALU.mult
                                                    ).then_inc(rden_step, 1)

                    def maxima(t, m):
                        nc.vector.tensor_reduce(
                            wmax24[:, t * NM + m:t * NM + m + 4],
                            wall32[:, bass.ds((t * (NM + 1) + m + 1) * SLOT, 4 * SLOT)].rearrange("p (k i) -> p k i", k=4),
                            AX.X, ALU.max, apply_absolute_value=True).then_inc(wmax_step, 1)

                    REST, STATS_AT = NT - EARLY, -1
                    for n in range(FIRST, SPLIT_AT):
                        if n == 0:
                            for b in range(2):
                                last = nc.vector.memset(vpair[b][:, :, :, :, :], 0.0)
                            last.then_inc(v_init, 1)
                            dve.wait_ge(v_init, 1)
                        for t in range(EARLY + 6 * (n - STATS_AT), min(EARLY + 6 * (n - STATS_AT + 1), NT)) if n >= STATS_AT else ():
                            if t % EARLY == 0:
                                dve.wait_ge(x_in[t // EARLY], 16)
                            nc.vector.bn_stats(stats[:, t, :], xs[:, t, :]).then_inc(rest_step, 1)
                        if n == REST_AT:
                            dve.wait_ge(rest_step, REST)
                            finish_stats(dve, rest_step, REST, slice(EARLY, NT), mean[:, EARLY:NT])
                        if n == REST_AT + 2:
                            finish_rstd(dve, rest_step, REST + STATS, 2, slice(EARLY, NT), rstd[:, EARLY:NT])
                        for i, at in enumerate((2, 4, 5)):
                            if n == at:
                                dve.wait_ge(w_in[i], 16 * NM if i < 2 else 16 * G4 * NI)
                                for k in range(2):
                                    maxima(i, 4 * k)
                                if i == 2:
                                    dve.wait_ge(wmax_step, 6)
                                    nc.vector.tensor_reduce(wmax[:, :], wmax24[:, :].rearrange("p (t m) -> p t m", m=NM), AX.X, ALU.max
                                                            ).then_inc(wmax_done, 1)
                        step(n, n)
                    dve.wait_ge(wmax_shared, 1)
                    nc.vector.tensor_scalar(pow2[:, :].bitcast(I32), wmax_all[:, :].bitcast(I32), 0x7F800000, None,
                                            ALU.bitwise_and).then_inc(scale_step, 1)
                    dve.wait_ge(scale_step, 1)
                    nc.vector.tensor_scalar(pow2[:, :], pow2[:, :], 2.0 ** -60, None, ALU.max).then_inc(scale_step, 1)
                    dve.wait_ge(scale_step, 2)
                    nc.vector.reciprocal(inv2[:, :], pow2[:, :]).then_inc(scale_step, 1)
                    dve.wait_ge(scale_step, 3)
                    nc.vector.tensor_scalar(wfac[:, :], inv2[:, 0:1], 0.125, None, ALU.mult).then_inc(scale_step, 1)
                    nc.vector.tensor_scalar(yfac[:, :], pow2[:, 0:1], pow2[:, 1:2], pow2[:, 2:3],
                                            ALU.mult, ALU.mult).then_inc(scale_step, 1)
                    dve.wait_ge(scale_step, 5)
                    nc.vector.tensor_scalar(yfac[:, :], yfac[:, :], 8.0, tanhg[:, 1:2], ALU.mult, ALU.mult
                                            ).then_inc(scale_step, 1)
                    dve.wait_ge(scale_step, 6)
                    for n in range(SPLIT_AT, LAST):
                        if n == SECOND_AT:
                            dve.wait_ge(stat_step, EARLY + STATS + RSTD + AHEAD)
                            finish_stats(dve, second_step, 0, slice(0, AHEAD), mean2[:, :])
                        step(n, n)
                        if n == SECOND_AT + 1:
                            finish_rstd(dve, second_step, STATS, 3, slice(0, AHEAD), rstd2[:, :])
                        for k in pieces(n - SPLIT_AT, 0, SPLIT, LATER):
                            lo(dve, k)

                @block.gpsimd
                def _(pool):
                    fill = nc.gpsimd.to_reg(MASKED)

                    def mask(j, b):
                        pool.wait_ge(s_copied, j + 1)
                        pool.sem_inc(mask_turn, 1)
                        for half in range(2):
                            v = sc[b][64 * half:64 * half + 64, :, :]
                            nc.gpsimd.affine_select(out=v, in_=v, compare_op=ALU.is_ge, fill=fill, base=0,
                                                    pattern=[[0, HEADS], [-1, S]], channel_multiplier=1
                                                    ).then_inc(masked, 1)

                    for j in range(SPLIT_AT - 1):
                        mask(j, j % 2)
                    pool.wait_ge(masked, 2 * (SPLIT_AT - 1))
                    pool.wait_ge(wmax_done, 1)
                    nc.gpsimd.partition_all_reduce(wmax_all[:, :], wmax[:, :], P, RMAX).then_inc(wmax_shared, 1)
                    pool.wait_ge(wmax_shared, 1)
                    assert NA == SPLIT_AT + 1
                    mask(SPLIT_AT - 1, (SPLIT_AT - 1) % 2)
                    pool.wait_ge(masked, 2 * SPLIT_AT)
                    pool.wait_ge(scale_step, 3)
                    for i in in_place[:3]:
                        scale(pool, i)
                    pool.wait_ge(scaled, 3)
                    mask(SPLIT_AT, SPLIT_AT % 2)
                    pool.wait_ge(masked, 2 * NA)
                    for i in in_place[3:]:
                        scale(pool, i)
                    pool.wait_ge(scaled, len(in_place))

        late = ExitStack()
        with late:
            xh = sbuf(late, "xh", [P, KT, RING * P], F16)
            xl = sbuf(late, "xl", [P, KT, RING * P], F16)
            wT = sbuf(late, "wT", [3 * E, RING * P], BF16)
            cum_run = sbuf(late, "cum_run", [P, E], BF16)
            with ExitStack() as phase:
                NR = AHEAD
                xn2 = [sbuf(phase, f"xn2_{i}", [P, D], F32) for i in range(2)]
                xTf = [sbuf(phase, f"xTf{i}", [P, KT, P], F32) for i in range(2)]
                lg = sbuf(phase, "lg", [P, NR, E], F32)
                lr = sbuf(phase, "lr", [P, NR, E], F32)
                ex = sbuf(phase, "ex", [P, NR, E], F32)
                mk = sbuf(phase, "mk", [P, NR, E], BF16)
                cum = sbuf(phase, "cum", [P, NR, E], BF16)
                w3 = sbuf(phase, "w3", [P, NR, 3, E], BF16)
                top = sbuf(phase, "top", [P, NR, TOP_K], F32)
                lmax = sbuf(phase, "lmax", [P, NR], F32)
                den = sbuf(phase, "den", [P, NR], F32)
                x_ps = [psum(phase, f"x_ps{i}", [P, 512], F32) for i in range(2)]
                lg_ps = psum(phase, "lg_ps", [P, NR, E], F32)
                pos_ps = psum(phase, "pos_ps", [P, NR, E], F32)
                wT_ps = psum(phase, "wT_ps", [P, 8 * P], BF16)

                n2_done, t2_done, f_done, hi_done, lo_done, lg_done = (sem(n) for n in (
                    "n2_done", "t2_done", "f_done", "hi_done", "lo_done", "lg_done"))
                r_step, e_done, cum_done, pos_done, w3_done, wt_done, wt_copied = (sem(n) for n in (
                    "r_step", "e_done", "cum_done", "pos_done", "w3_done", "wt_done", "wt_copied"))

                with nc.Block() as block:
                    @block.vector
                    def _(dve):
                        def norm(t, b):
                            wait(dve, t2_done, t - 1)
                            nc.vector.tensor_scalar(xn2[b][:, :], xs[:, bass.ds(t, 1), :], mean2[:, t:t + 1],
                                                    rstd2[:, t:t + 1], ALU.subtract, ALU.mult
                                                    ).then_inc(n2_done, 1)

                        def low(t, b):
                            wait(dve, hi_done, t + 1)
                            at = bass.ds(t * P, P)
                            nc.vector.tensor_tensor(xl[:, :, at], x_ps[b][:, 0:KT * P].rearrange("p (c n) -> p c n", c=KT),
                                                    xh[:, :, at], ALU.subtract).then_inc(lo_done, 1)

                        norm(0, 0)
                        norm(1, 1)
                        for t in range(NR):
                            low(t, t % 2)
                            if t + 2 < NR:
                                norm(t + 2, t % 2)

                        count = [0]

                        def step(instruction):
                            count[0] += 1
                            instruction.then_inc(r_step, 1)
                            dve.wait_ge(r_step, count[0])

                        def over_e(v):
                            return v[:, :, None].to_broadcast([P, NR, E])

                        dve.wait_ge(lg_done, NR)
                        step(nc.vector.tensor_reduce(lmax[:, :], lg_ps[:, :, :], AX.X, ALU.max))
                        step(nc.vector.tensor_tensor(lg[:, :, :], lg_ps[:, :, :], over_e(lmax), ALU.subtract))
                        step(nc.vector.tensor_scalar(lg[:, :, :], lg[:, :, :], EXP_FLOOR, None, ALU.max))
                        for t in range(NR):
                            last = nc.vector.max(top[:, t, :], lg[:, t, :])
                        step(last)
                        for t in range(NR):
                            last = nc.vector.match_replace(lr[:, t, :], top[:, t, :], lg[:, t, :], -1e30)
                        step(last)
                        step(nc.vector.tensor_tensor(mk[:, :, :], lr[:, :, :], lg[:, :, :], ALU.not_equal))
                        dve.wait_ge(e_done, 1)
                        step(nc.vector.tensor_tensor(ex[:, :, :], ex[:, :, :], mk[:, :, :], ALU.mult))
                        step(nc.vector.tensor_reduce(den[:, :], ex[:, :, :], AX.X, ALU.add))
                        step(nc.vector.reciprocal(den[:, :], den[:, :]))
                        step(nc.vector.tensor_tensor(ex[:, :, :], ex[:, :, :], over_e(den), ALU.mult))
                        dve.wait_ge(pos_done, 1)
                        step(nc.vector.scalar_tensor_tensor(ex[:, :, :], pos_ps[:, :, :], float(CAP), ex[:, :, :],
                                                            ALU.is_lt, ALU.mult))
                        step(nc.vector.tensor_scalar(ex[:, :, :], ex[:, :, :], wfac[:, 0:1], None, ALU.mult))
                        for part in range(3):
                            step(nc.vector.tensor_copy(w3[:, :, part, :], ex[:, :, :]))
                            if part < 2:
                                step(nc.vector.tensor_tensor(ex[:, :, :], ex[:, :, :], w3[:, :, part, :],
                                                             ALU.subtract))
                        nc.vector.engine_nop().then_inc(w3_done, 1)
                        dve.wait_ge(cum_done, NR)
                        nc.vector.tensor_tensor(cum_run[:, :], cum[:, NR - 1, :], mk[:, NR - 1, :], ALU.add
                                                ).then_inc(cum_done, 1)
                        dve.wait_ge(wt_done, 1)
                        nc.vector.tensor_copy(wT[:, 0:NR * P], wT_ps[0:3 * E, 0:NR * P]).then_inc(wt_copied, 1)
                        dve.wait_ge(wt_copied, 1)
                        dve.wait_ge(cum_done, NR + 1)

                    @block.tensor
                    def _(pe):
                        def transpose(t, b):
                            wait(pe, n2_done, t + 1)
                            wait(pe, f_done, t - 1)
                            wait(pe, lo_done, t - 1)
                            for c in range(KT):
                                last = nc.tensor.transpose(x_ps[b][:, c * P:(c + 1) * P],
                                                           xn2[b][:, c * P:(c + 1) * P], identf[:, :])
                            last.then_inc(t2_done, 1)

                        def gate(t, b):
                            wait(pe, f_done, t + 1)
                            for c in range(KT):
                                last = nc.tensor.matmul(lg_ps[:, bass.ds(t, 1), :], xTf[b][:, c, :], gatew[:, c, :],
                                                        start=(c == 0), stop=(c == KT - 1))
                            last.then_inc(lg_done, 1)

                        transpose(0, 0)
                        for t in range(NR):
                            if t + 1 < NR:
                                transpose(t + 1, (t + 1) % 2)
                            gate(t, t % 2)
                        pe.wait_ge(r_step, 6)
                        pe.wait_ge(cum_done, NR)
                        nc.tensor.matmul(pos_ps[:, :, :], tri[:, :], mk[:, :, :], start=True, stop=False)
                        nc.tensor.matmul(pos_ps[:, :, :], onesb[:, :], cum[:, :, :], start=False, stop=True
                                         ).then_inc(pos_done, 1)
                        pe.wait_ge(w3_done, 1)
                        for t in range(NR):
                            last = nc.tensor.transpose(wT_ps[0:3 * E, t * P:(t + 1) * P],
                                                       w3[:, t, :, :].rearrange("p a e -> p (a e)"), identb[:, :])
                        last.then_inc(wt_done, 1)

                    @block.scalar
                    def _(act):
                        def copies(t, b):
                            wait(act, t2_done, t + 1)
                            wait(act, lg_done, t - 1)
                            src = x_ps[b][:, 0:KT * P].rearrange("p (c n) -> p c n", c=KT)
                            nc.scalar.activation(xTf[b][:, :, :], src, ACT.Copy).then_inc(f_done, 1)
                            nc.scalar.activation(xh[:, :, bass.ds(t * P, P)], src, ACT.Copy).then_inc(hi_done, 1)
                        for t in range(NR):
                            copies(t, t % 2)
                        act.wait_ge(r_step, 3)
                        nc.scalar.activation(ex[:, :, :], lg[:, :, :], ACT.Exp).then_inc(e_done, 1)

                    @block.gpsimd
                    def _(pool):
                        nc.gpsimd.memset(cum[:, 0, :], 0.0).then_inc(cum_done, 1)
                        pool.wait_ge(r_step, 6)
                        for t in range(1, NR):
                            pool.wait_ge(cum_done, t)
                            nc.gpsimd.tensor_tensor(cum[:, t, :], cum[:, t - 1, :], mk[:, t - 1, :], ALU.add
                                                    ).then_inc(cum_done, 1)

            with ExitStack() as phase:
                NS = (T // NB) * (NM // 2)
                SPB = NM // 2
                CH = 2 * NI
                assert NS == NT and SPB == TPB
                ysum = sbuf(phase, "ysum", [P, KT, RING * P], F32)
                sg = [sbuf(phase, f"sg{i}", [P, NB], F32) for i in range(2)]
                wb = [sbuf(phase, f"wb{i}", [P, NB], F32) for i in range(2)]
                hf = [sbuf(phase, f"hf{i}", [P, NB], F32) for i in range(2)]
                hh = [sbuf(phase, f"hh{i}", [P, NB], F16) for i in range(NI)]
                hl = [sbuf(phase, f"hl{i}", [P, NB], F16) for i in range(NI)]
                yt = sbuf(phase, "yt", [P, KT, P], F32)
                xn2 = sbuf(phase, "xn2b", [P, D], F32)
                xTf = sbuf(phase, "xTfb", [P, KT, P], F32)
                lg = sbuf(phase, "lgb", [P, E], F32)
                lr = sbuf(phase, "lrb", [P, E], F32)
                ex = sbuf(phase, "exb", [P, E], F32)
                mk = sbuf(phase, "mkb", [P, E], BF16)
                w3 = sbuf(phase, "w3b", [P, 3, E], BF16)
                top = sbuf(phase, "topb", [P, TOP_K], F32)
                lmax = sbuf(phase, "lmaxb", [P, 1], F32)
                den = sbuf(phase, "denb", [P, 1], F32)
                mv = sbuf(phase, "mv", [P, 8], F32)
                stat = sbuf(phase, "stat", [P, 6], F32)
                spare = sbuf(phase, "spare", [P, 3], F32)
                none = sbuf(phase, "none", [P, KT, P], F32)
                cnat = sbuf(phase, "cnat_s", [P, D], F32)
                cdup = sbuf(phase, "cdup_s", [P, 2, D], F32)
                xn = sbuf(phase, "xn_s", [P, D], F32)
                qT = sbuf(phase, "qT_s", [P, KT, P], F32)
                kpair = sbuf(phase, "kpair_s", [P, KT * 2, 2, S], F32)
                sc = sbuf(phase, "sc_s", [P, HEADS, S], F32)
                pr = sbuf(phase, "pr_s", [P, HEADS * S], F32)
                pT = sbuf(phase, "pT_s", [P, HEADS // 2, P], F32)
                vpair = sbuf(phase, "vpair_s", [P, 2, HEADS // 2, 2, HD], F32)
                oT = sbuf(phase, "oT_s", [P, KT, P], F32)
                smax = sbuf(phase, "smax_s", [P, HEADS], F32)
                aden = sbuf(phase, "aden_s", [P, HEADS], F32)
                rden = sbuf(phase, "rden_s", [P, HEADS], F32)
                att = sbuf(phase, "att_s", [P, HEADS, HD], F32)
                g_ps = [psum(phase, f"g_ps{i}", [P, NB], F32) for i in range(2)]
                u_ps = [psum(phase, f"u_ps{i}", [P, NB], F32) for i in range(2)]
                b_ps = psum(phase, "b_ps", [P, NB], F32)
                y_ps = psum(phase, "y_ps", [P, KT, NB], F32)
                r_ps = psum(phase, "r_ps", [P, 512], F32)
                turned = r_ps[:, 0:KT * P]
                lg_ps = r_ps[:, KT * P:KT * P + E]
                pos_ps = r_ps[:, KT * P + E:KT * P + 2 * E]
                wT_ps = r_ps[:, KT * P + 2 * E:KT * P + 2 * E + P // 2].bitcast(BF16)[0:3 * E, :]

                gu_done, silu_done, wb_made, wb_copied, sgw_done = (sem(n) for n in (
                    "gu_done", "silu_done", "wb_made", "wb_copied", "sgw_done"))
                h_done, hh_done, hl_done, down_done, y_added = (sem(n) for n in (
                    "h_done", "hh_done", "hl_done", "down_done", "y_added"))
                yt_done, ft_done, fin_done, stored = sem("yt_done"), sem("ft_done"), sem("fin_done"), sem("stored")
                rn_done, rt_done, rf_done, rhi_done, rlo_done, rlg_done = (sem(n) for n in (
                    "rn_done", "rt_done", "rf_done", "rhi_done", "rlo_done", "rlg_done"))
                rexp_done, rpos_done, rwt_done, rwt_copied = (sem(n) for n in (
                    "rexp_done", "rpos_done", "rwt_done", "rwt_copied"))
                a_load, a_cdup, a_norm, a_tqk, a_q, a_k, a_s, a_sc, a_mask, a_turn, a_max, a_sub = (sem(n) for n in (
                    "a_load", "a_cdup", "a_norm", "a_tqk", "a_q", "a_k", "a_s", "a_sc", "a_mask", "a_turn",
                    "a_max", "a_sub"))
                a_exp, a_tp, a_pT, a_v, a_vinit, a_den, a_pv, a_oT, a_o, a_att, a_x1 = (sem(n) for n in (
                    "a_exp", "a_tp", "a_pT", "a_v", "a_vinit", "a_den", "a_pv", "a_oT", "a_o", "a_att", "a_x1"))
                chain_n, a_stat, zeroed = sem("chain_n"), sem("a_stat"), sem("zeroed")
                LATE = ((3 * NM - LATER) // 3,) * 3
                assert LATER >= 12 and max(LATE) <= CH
                GROUPS = KT * G4
                NEWTON = 3
                STAT_STEPS, D_STEPS = 7 + 2 * NEWTON, 3
                chain_a, chain_b, carried = sem("chain_a"), sem("chain_b"), sem("carried")
                A_STEPS, B_STEPS = 5, 12

                def turns(s):
                    return -1 <= s < NT - NA - 1

                def scores(s):
                    return 0 <= s < NT - NA

                def exps(s):
                    return 1 <= s < NT - NA + 1

                def values(s):
                    return 2 <= s < NT - AHEAD

                def routes(s):
                    return 0 <= s < NT - AHEAD

                def results(s):
                    return s >= AHEAD

                def over_steps(engine, step, pairs=False):
                    def one_by_one(first, end):
                        for s in range(first, end):
                            step(s, s)

                    def alike(first, end):
                        if pairs and (end - first) % 2 == 0:
                            with engine.Fori(first, end - 1, 2) as s:
                                step(s, first)
                                step(s + 1, first)
                        else:
                            with engine.Fori(first, end) as s:
                                step(s, first)
                    one_by_one(0, 3)
                    alike(3, AHEAD)
                    one_by_one(AHEAD, AHEAD + 1)
                    alike(AHEAD + 1, NT - NA - 1)
                    one_by_one(NT - NA - 1, NT - AHEAD + 1)
                    alike(NT - AHEAD + 1, NS - 1)
                    one_by_one(NS - 1, NS)

                def late_piece(k, j):
                    first = LATER + sum(LATE[:k])
                    return [first + j] if k < len(LATE) and j < LATE[k] else []

                def ring(t):
                    return (t % RING if isinstance(t, int) else nc.s_assert_within(
                        t & (RING - 1), 0, RING - 1, skip_runtime_bounds_check_because="masked")) * P

                def ring_block(s):
                    b = block_of(s)
                    return (b % (RING // TPB) if isinstance(b, int) else nc.s_assert_within(
                        b & (RING // TPB - 1), 0, RING // TPB - 1, skip_runtime_bounds_check_because="masked")) * NB

                def q_parts():
                    return b_ps[:, KT * P:2 * KT * P].rearrange("p (c h s) -> p (c h) s", c=KT, h=2)

                def block_of(s):
                    return s // SPB if isinstance(s, int) else nc.s_assert_within(
                        s >> 2, 0, T // NB - 1, skip_runtime_bounds_check_because="the loop ends at NS")

                def pair_of(s):
                    return s % SPB if isinstance(s, int) else nc.s_assert_within(
                        s & 3, 0, SPB - 1, skip_runtime_bounds_check_because="the loop ends at NS")

                with nc.Block() as block:
                    @block.tensor
                    def _(pe):
                        def spread(s, a, routed=0):
                            m = 2 * s + a
                            wait(pe, wb_copied, m)
                            wait(pe, rwt_copied, routed)
                            nc.tensor.matmul(b_ps[:, :], sel[:, bass.ds(2 * pair_of(s) + a, 1), :],
                                             wT[:, bass.ds(ring_block(s), NB)], start=True, stop=True
                                             ).then_inc(wb_made, 1)

                        def gate_up(s, j, between=()):
                            c = CH * s + j
                            wait(pe, silu_done, c - 1)
                            wait(pe, h_done, c - 1)
                            tok = ring_block(s)
                            between = list(between)
                            for n, dst in ((0, g_ps), (1, u_ps)):
                                base = (pair_of(s) * 2 + (n * (NM + 1) + j // NI)) * (2 * SLOT) + (j % NI) * P
                                terms = [(part, xp, half) for half in range(KT) for part, xp in
                                         ((0, xh), (0, xl), (1, xh))]
                                for i, (part, xp, half) in enumerate(terms):
                                    last = nc.tensor.matmul(
                                        dst[j % 2][:, :], wall[:, bass.ds(base + part * SLOT + half * NI * P, P)],
                                        xp[:, half, bass.ds(tok, NB)], start=(i == 0), stop=(i == len(terms) - 1))
                                    if i % 3 == 1 and between:
                                        between.pop(0)()
                            last.then_inc(gu_done, 1)

                        def down(s, j):
                            c = CH * s + j
                            wait(pe, hl_done, c + 1)
                            if j == 0:
                                wait(pe, y_added, s + 1)
                            base = (pair_of(s) * 2 + (2 * (NM + 1) + j // NI)) * (2 * SLOT) + (j % NI) * D
                            for half in range(KT):
                                for i, (part, hp) in enumerate(((0, hh), (0, hl), (1, hh))):
                                    last = nc.tensor.matmul(
                                        y_ps[:, half, :], wall[:, bass.ds(base + part * SLOT + half * P, P)],
                                        hp[j % NI][:, :], start=(j == 0 and i == 0), stop=(j == CH - 1 and i == 2))
                            last.then_inc(down_done, 1)

                        def turn_result(f, s, k):
                            wait(pe, yt_done, f + 1)
                            wait(pe, rwt_copied, s if k <= NT - AHEAD else NT - AHEAD)
                            if values(k):
                                wait(pe, a_att, s - 1)
                            wait(pe, fin_done, f)
                            for c in range(KT):
                                last = nc.tensor.transpose(turned[:, c * P:(c + 1) * P], yt[:, c, :], identf[:, :])
                            last.then_inc(ft_done, 1)

                        def route_x(s, k):
                            wait(pe, rn_done, s + 1)
                            wait(pe, rwt_copied, s)
                            if values(k):
                                wait(pe, a_att, s - 1)
                            if results(k):
                                wait(pe, fin_done, s - AHEAD + 1)
                            for c in range(KT):
                                last = nc.tensor.transpose(turned[:, c * P:(c + 1) * P], xn2[:, c * P:(c + 1) * P],
                                                           identf[:, :])
                            last.then_inc(rt_done, 1)

                        def route_gate(s):
                            wait(pe, rf_done, s + 1)
                            wait(pe, rlo_done, s + 1)
                            for c in range(KT):
                                last = nc.tensor.matmul(lg_ps, xTf[:, c, :], gatew[:, c, :],
                                                        start=(c == 0), stop=(c == KT - 1))
                            last.then_inc(rlg_done, 1)

                        def route_places(s):
                            wait(pe, chain_a, A_STEPS * (s + 1))
                            nc.tensor.matmul(pos_ps, tri[:, :], mk[:, :], start=True, stop=False)
                            nc.tensor.matmul(pos_ps, onesb[:, :], cum_run[:, :], start=False, stop=True
                                             ).then_inc(rpos_done, 1)

                        def route_weights(s):
                            wait(pe, chain_b, B_STEPS * (s + 1))
                            nc.tensor.transpose(wT_ps, w3[:, :, :].rearrange("p a e -> p (a e)"), identb[:, :]
                                                ).then_inc(rwt_done, 1)

                        def turn_qk(s):
                            a = s + 1
                            wait(pe, a_norm, a + 1)
                            wait(pe, a_load, 16 * (a + 1))
                            for c in range(KT):
                                nc.tensor.transpose(b_ps[:, c * P:(c + 1) * P], xn[:, c * P:(c + 1) * P], identf[:, :])
                            for c in range(KT):
                                last = nc.tensor.transpose(b_ps[:, (KT + c) * P:(KT + c + 1) * P],
                                                           cnat[:, c * P:(c + 1) * P], identf[:, :])
                            last.then_inc(a_tqk, 1)

                        def score(s, c):
                            def group(g):
                                def issue():
                                    if g == 0:
                                        wait(pe, a_q, s + 1)
                                        wait(pe, wb_copied, 2 * s + 2) if c == 0 else wait(pe, a_sc, 2 * s + 1)
                                    else:
                                        wait(pe, a_s, GROUPS * s + c * G4 + g)
                                    rows = slice(32 * g, 32 * g + 32)
                                    for h in range(2):
                                        last = nc.tensor.matmul(
                                            b_ps[64 * h:64 * h + 64, g * P:(g + 1) * P],
                                            qT[rows, c, 64 * h:64 * h + 64],
                                            kpair[rows, 2 * c + h, :, :].rearrange("p a s -> p (a s)"),
                                            start=True, stop=True)
                                    last.then_inc(a_s, 1)
                                return issue
                            return [group(g) for g in range(G4)]

                        def turn_exp(s, half):
                            a = s - 1
                            wait(pe, a_exp, a + 1)
                            wait(pe, wb_copied, 2 * s + 3) if half == 0 else wait(pe, a_pT, 2 * a + 1)
                            for i in range(4):
                                c = 4 * half + i
                                last = nc.tensor.transpose(b_ps[:, i * P:(i + 1) * P], pr[:, c * P:(c + 1) * P],
                                                           identf[:, :])
                            last.then_inc(a_tp, 1)

                        def value(s):
                            a = s - 2
                            wait(pe, a_pT, 2 * a + 2)
                            wait(pe, a_v, a + 1)
                            wait(pe, rwt_copied, s)
                            for h in range(2):
                                for pair in range(HEADS // 2):
                                    c, g = pair // G4, pair % G4
                                    last = nc.tensor.matmul(
                                        r_ps[32 * g:32 * g + 32, c * P + 64 * h:c * P + 64 * h + 64],
                                        vpair[:, h, pair, :, :].rearrange("p a d -> p (a d)"),
                                        pT[:, pair, 64 * h:64 * h + 64], start=True, stop=True)
                            last.then_inc(a_pv, 1)

                        def turn_value(s):
                            wait(pe, a_oT, s - 1)
                            for c in range(KT):
                                last = nc.tensor.transpose(r_ps[:, (KT + c) * P:(KT + c + 1) * P], oT[:, c, :],
                                                           identf[:, :])
                            last.then_inc(a_o, 1)

                        def step(s, k):
                            more = k + 1 < NS
                            gate_up(s, 2)
                            if values(k):
                                value(s)
                            down(s, 0)
                            if values(k):
                                turn_value(s)
                            if scores(k):
                                wait(pe, a_q, s + 1)
                                wait(pe, a_k, s + 1)
                            if exps(k - 1):
                                wait(pe, a_pT, 2 * (s - 1))
                            spread(s, 1)
                            gate_up(s, 3)
                            down(s, 1)
                            if results(k):
                                turn_result(s - AHEAD, s, k)
                            gate_up(s, 4, score(s, 0) if scores(k) else ())
                            down(s, 2)
                            if routes(k):
                                route_x(s, k)
                            gate_up(s, 5, score(s, 1) if scores(k) else ())
                            if routes(k):
                                route_gate(s)
                            down(s, 3)
                            if more:
                                if scores(k):
                                    wait(pe, a_sc, 2 * s + 2)
                                spread(s + 1, 0, s if k <= NT - AHEAD else NT - AHEAD)
                                if k < len(LATE):
                                    wait(pe, lo_split, 6 * (k + 2))
                                gate_up(s + 1, 0)
                            if routes(k):
                                route_places(s)
                            down(s, 4)
                            if exps(k):
                                turn_exp(s, 0)
                            if more:
                                gate_up(s + 1, 1)
                            if exps(k):
                                turn_exp(s, 1)
                            if routes(k):
                                route_weights(s)
                            down(s, 5)
                            if turns(k):
                                wait(pe, a_pT, 2 * s) if exps(k) else wait(pe, wb_copied, 2 * s + 3)
                                turn_qk(s)

                        spread(0, 0)
                        gate_up(0, 0)
                        gate_up(0, 1)
                        wait(pe, wb_copied, 1)
                        turn_qk(-1)
                        over_steps(nc.tensor, step, pairs=True)
                        for f in range(NT - AHEAD, NT):
                            turn_result(f, NS, NS)

                    @block.scalar
                    def _(act):
                        def copy_wb(s, a):
                            wait(act, wb_made, 2 * s + a + 1)
                            wait(act, sgw_done, CH * (s - 1) + NI * (a + 1))
                            nc.scalar.activation(wb[a][:, :], b_ps[:, :], ACT.Copy).then_inc(wb_copied, 1)

                        def silu(s, j):
                            c = CH * s + j
                            wait(act, gu_done, c + 1)
                            wait(act, h_done, c - 1)
                            nc.scalar.activation(sg[j % 2][:, :], g_ps[j % 2][:, :], ACT.Silu, scale=pow2[:, 0:1]
                                                 ).then_inc(silu_done, 1)

                        def split_hi(s, j, k):
                            c = CH * s + j
                            wait(act, h_done, c + 1)
                            wait(act, down_done, c - 2)
                            nc.scalar.activation(hh[j % NI][:, :], hf[j % 2][:, :], ACT.Copy).then_inc(hh_done, 1)
                            for i in late_piece(k, j):
                                hi(act, i)

                        def take_sum(f):
                            wait(act, y_added, min(f + AHEAD, NS + 1) if isinstance(f, int) else f + AHEAD)
                            wait(act, ft_done, f)
                            nc.scalar.activation(yt[:, :, :], ysum[:, :, bass.ds(ring(f), P)], ACT.Copy
                                                 ).then_inc(yt_done, 1)

                        def table(i, function):
                            nc.scalar.activation(spare[:, i:i + 1], parity[:, 0:1], function)

                        def copy_exp(s, half):
                            a = s - 2
                            wait(act, a_tp, 2 * a + half + 1)
                            if half == 0:
                                wait(act, a_pv, a)
                            nc.scalar.activation(pT[:, 4 * half:4 * half + 4, :],
                                                 b_ps[:, :].rearrange("p (c n) -> p c n", n=P), ACT.Copy
                                                 ).then_inc(a_pT, 1)

                        def copy_scores(s, c):
                            wait(act, a_s, GROUPS * s + G4 * (c + 1))
                            if c == 0:
                                wait(act, a_exp, s)
                            n = HEADS // KT
                            nc.scalar.activation(sc[:, c * n:(c + 1) * n, :],
                                                 b_ps[:, :].rearrange("p (h s) -> p h s", s=S), ACT.Copy,
                                                 scale=HD ** -0.5).then_inc(a_sc, 1)

                        def step(s, k):
                            silu(s, 0)
                            if values(k):
                                copy_exp(s, 0)
                            split_hi(s, 0, k)
                            if values(k):
                                copy_exp(s, 1)
                            silu(s, 1)
                            if exps(k):
                                table(0, ACT.Exp)
                                wait(act, a_sub, s)
                                wait(act, a_tp, 2 * (s - 1))
                                wait(act, a_den, D_STEPS * (s - 1))
                                nc.scalar.activation(pr[:, :], sc[:, :, :].rearrange("p h s -> p (h s)"), ACT.Exp
                                                     ).then_inc(a_exp, 1)
                                table(1, ACT.Silu)
                            split_hi(s, 1, k)
                            if scores(k):
                                wait(act, a_k, s + 1)
                                nc.scalar.activation(qT[:, :, :], b_ps[:, 0:KT * P].rearrange("p (c n) -> p c n", c=KT),
                                                     ACT.Copy).then_inc(a_q, 1)
                            if values(k):
                                wait(act, a_pv, s - 1)
                                wait(act, a_o, s - 2)
                                nc.scalar.activation(oT[:, :, :], turned.rearrange("p (c n) -> p c n", c=KT), ACT.Copy
                                                     ).then_inc(a_oT, 1)
                            silu(s, 2)
                            copy_wb(s, 1)
                            split_hi(s, 2, k)
                            if results(k):
                                take_sum(s - AHEAD)
                            silu(s, 3)
                            split_hi(s, 3, k)
                            if scores(k):
                                copy_scores(s, 0)
                            silu(s, 4)
                            if routes(k):
                                wait(act, rt_done, s + 1)
                                wait(act, rlg_done, s)
                                src = turned.rearrange("p (c n) -> p c n", c=KT)
                                nc.scalar.activation(xTf[:, :, :], src, ACT.Copy).then_inc(rf_done, 1)
                                nc.scalar.activation(xh[:, :, bass.ds(ring(s + AHEAD), P)], src, ACT.Copy
                                                     ).then_inc(rhi_done, 1)
                            split_hi(s, 4, k)
                            if scores(k):
                                copy_scores(s, 1)
                            silu(s, 5)
                            if routes(k):
                                wait(act, chain_a, A_STEPS * s + 2)
                                wait(act, chain_b, B_STEPS * s)
                                nc.scalar.activation(ex[:, :], lg[:, :], ACT.Exp).then_inc(rexp_done, 1)
                                table(2, ACT.Silu)
                            split_hi(s, 5, k)
                            if k + 1 < NS:
                                copy_wb(s + 1, 0)

                        copy_wb(0, 0)
                        over_steps(nc.scalar, step)
                        for f in range(NT - AHEAD, NT):
                            take_sum(f)

                    @block.gpsimd
                    def _(pool):
                        fill = nc.gpsimd.to_reg(MASKED)
                        nc.gpsimd.memset(none[:, :, :], 0.0)
                        nc.gpsimd.memset(ysum[:, :, :], 0.0).then_inc(y_added, 1)
                        pool.wait_ge(y_added, 1)
                        pool.sem_inc(zeroed, RING)

                        def step(s, k):
                            for j in range(CH):
                                c = CH * s + j
                                pool.wait_ge(silu_done, c + 1)
                                if j % NI == 0:
                                    pool.wait_ge(wb_copied, 2 * s + j // NI + 1)
                                nc.gpsimd.tensor_tensor(sg[j % 2][:, :], sg[j % 2][:, :], wb[j // NI][:, :], ALU.mult
                                                        ).then_inc(sgw_done, 1)
                                if j == 4 and results(k):
                                    pool.wait_ge(yt_done, s - AHEAD + 1)
                                    nc.gpsimd.tensor_copy(ysum[:, :, bass.ds(ring(s - AHEAD), P)], none[:, :, :]
                                                          ).then_inc(zeroed, 1)
                            if scores(k):
                                pool.wait_ge(sgw_done, CH * (s + 1))
                                pool.wait_ge(a_sc, 2 * s + 2)
                                if results(k):
                                    pool.wait_ge(zeroed, RING + s - AHEAD + 1)
                                pool.sem_inc(a_turn, 1)
                                for half in range(2):
                                    v = sc[64 * half:64 * half + 64, :, :]
                                    nc.gpsimd.affine_select(out=v, in_=v, compare_op=ALU.is_ge, fill=fill, base=0,
                                                            pattern=[[0, HEADS], [-1, S]], channel_multiplier=1
                                                            ).then_inc(a_mask, 1)
                                pool.wait_ge(a_mask, 2 * s + 2)
                        over_steps(nc.gpsimd, step)

                    @block.vector
                    def _(dve):
                        def hidden(s, j):
                            c = CH * s + j
                            wait(dve, sgw_done, c + 1)
                            wait(dve, hl_done, c - 1)
                            nc.vector.tensor_tensor(hf[j % 2][:, :], sg[j % 2][:, :], u_ps[j % 2][:, :], ALU.mult
                                                    ).then_inc(h_done, 1)

                        def split_lo(s, j, k):
                            c = CH * s + j
                            wait(dve, hh_done, c + 1)
                            wait(dve, down_done, c - 2)
                            nc.vector.tensor_tensor(hl[j % NI][:, :], hf[j % 2][:, :], hh[j % NI][:, :], ALU.subtract
                                                    ).then_inc(hl_done, 1)
                            for i in late_piece(k, j):
                                lo(dve, i)

                        def add(s):
                            wait(dve, down_done, CH * (s + 1))
                            wait(dve, y_added, s + 1)
                            wait(dve, zeroed, s + 4)
                            v = ysum[:, :, bass.ds(ring_block(s), NB)]
                            nc.vector.tensor_tensor(v, v, y_ps[:, :, :], ALU.add).then_inc(y_added, 1)

                        def result_row(f):
                            wait(dve, ft_done, f + 1)
                            row = xs[:, bass.ds(f, 1), :]
                            nc.vector.scalar_tensor_tensor(row, turned[:, None, :], yfac[:, 0:1], row,
                                                           ALU.mult, ALU.add).then_inc(fin_done, 1)

                        def norm(s, k):
                            wait(dve, rt_done, s)
                            t = s + AHEAD
                            wait(dve, chain_n, STAT_STEPS * (s + 1))
                            nc.vector.tensor_scalar(xn2[:, :], xs[:, bass.ds(t, 1), :], mv[:, 0:1], mv[:, 5:6],
                                                    ALU.subtract, ALU.mult).then_inc(rn_done, 1)

                        def route_lo(s):
                            wait(dve, rhi_done, s + 1)
                            at = bass.ds(ring(s + AHEAD), P)
                            nc.vector.tensor_tensor(xl[:, :, at], turned.rearrange("p (c n) -> p c n", c=KT),
                                                    xh[:, :, at], ALU.subtract).then_inc(rlo_done, 1)

                        def chained(signal, steps, s):
                            count = [0]

                            def link(instruction):
                                count[0] += 1
                                instruction.then_inc(signal, 1)
                                wait(dve, signal, steps * s + count[0])
                            return link

                        def pick(s):
                            link = chained(chain_a, A_STEPS, s)
                            wait(dve, rlg_done, s + 1)
                            wait(dve, rexp_done, s)
                            link(nc.vector.tensor_reduce(lmax[:, :], lg_ps, AX.X, ALU.max))
                            link(nc.vector.tensor_scalar(lg[:, :], lg_ps, lmax[:, 0:1], EXP_FLOOR,
                                                         ALU.subtract, ALU.max))
                            dve.sem_inc(carried, 1)
                            link(nc.vector.max(top[:, :], lg[:, :]))
                            dve.sem_inc(carried, 1)
                            link(nc.vector.match_replace(lr[:, :], top[:, :], lg[:, :], -1e30))
                            wait(dve, rpos_done, s)
                            link(nc.vector.tensor_tensor(mk[:, :], lr[:, :], lg[:, :], ALU.not_equal))

                        def weigh(s):
                            link = chained(chain_b, B_STEPS, s)
                            wait(dve, rexp_done, s + 1)
                            link(nc.vector.tensor_tensor(ex[:, :], ex[:, :], mk[:, :], ALU.mult))
                            link(nc.vector.tensor_reduce(den[:, :], ex[:, :], AX.X, ALU.add))
                            link(nc.vector.reciprocal(den[:, :], den[:, :]))
                            link(nc.vector.tensor_scalar(ex[:, :], ex[:, :], den[:, 0:1], None, ALU.mult))
                            wait(dve, rpos_done, s + 1)
                            link(nc.vector.scalar_tensor_tensor(ex[:, :], pos_ps, float(CAP), ex[:, :],
                                                                ALU.is_lt, ALU.mult))
                            link(nc.vector.tensor_scalar(ex[:, :], ex[:, :], wfac[:, 0:1], None, ALU.mult))
                            wait(dve, rwt_done, s)
                            for part in range(3):
                                link(nc.vector.tensor_copy(w3[:, part, :], ex[:, :]))
                                if part < 2:
                                    link(nc.vector.tensor_tensor(ex[:, :], ex[:, :], w3[:, part, :], ALU.subtract))
                            link(nc.vector.tensor_tensor(cum_run[:, :], cum_run[:, :], mk[:, :], ALU.add))

                        def copy_weights(s):
                            wait(dve, rwt_done, s + 1)
                            nc.vector.tensor_copy(wT[:, bass.ds(ring(s + AHEAD), P)], wT_ps).then_inc(rwt_copied, 1)

                        def take_k(s):
                            wait(dve, a_tqk, s + 1)
                            wait(dve, a_s, GROUPS * s)
                            nc.vector.tensor_tensor(
                                kpair[:, :, :, :], q_parts()[:, :, None, :].to_broadcast([P, 2 * KT, 2, S]),
                                parity[:, None, :, None].to_broadcast([P, 2 * KT, 2, S]), ALU.mult).then_inc(a_k, 1)

                        def norm_q(s):
                            t = s + NA + 1
                            wait(dve, a_tqk, s + 1)
                            nc.vector.tensor_scalar(xn[:, :], xs[:, bass.ds(t, 1), :], mean[:, bass.ds(t, 1)],
                                                    rstd[:, bass.ds(t, 1)], ALU.subtract, ALU.mult
                                                    ).then_inc(a_norm, 1)

                        def maximum(s):
                            wait(dve, a_mask, 2 * s)
                            wait(dve, a_sub, s - 1)
                            nc.vector.tensor_reduce(smax[:, :], sc[:, :, :], AX.X, ALU.max).then_inc(a_max, 1)

                        def less_maximum(s):
                            wait(dve, a_max, s)
                            nc.vector.tensor_tensor(sc[:, :, :], sc[:, :, :], smax[:, :, None].to_broadcast([P, HEADS, S]),
                                                    ALU.subtract).then_inc(a_sub, 1)

                        def denominators(s):
                            link = chained(a_den, D_STEPS, s - 1)
                            wait(dve, a_exp, s)
                            wait(dve, a_att, s - 2)
                            link(nc.vector.tensor_reduce(aden[:, :], pr[:, :].rearrange("p (h s) -> p h s", s=S), AX.X,
                                                         ALU.add))
                            link(nc.vector.reciprocal(rden[:, :], aden[:, :]))
                            link(nc.vector.tensor_scalar(rden[:, :], rden[:, :], tanhg[:, 0:1], None, ALU.mult))

                        def spread_values(s):
                            wait(dve, a_cdup, 32 * s)
                            wait(dve, a_pv, s - 1)
                            src = cdup[:, :, :].rearrange("p h (c a d) -> p h c a d", a=2, d=HD)
                            for half in range(2):
                                rows = slice(64 * half, 64 * half + 64)
                                last = nc.vector.tensor_copy(vpair[rows, :, :, half, 0:HD], src[rows, :, :, half, :])
                            last.then_inc(a_v, 1)

                        def attend(s):
                            a = s - 2
                            row = xs[:, bass.ds(s + AHEAD, 1), :]
                            wait(dve, a_o, a + 1)
                            nc.vector.tensor_tensor(att[:, :, :], r_ps[:, KT * P:2 * KT * P].rearrange(
                                "p (h d) -> p h d", d=HD), rden[:, :, None].to_broadcast([P, HEADS, HD]), ALU.mult
                                ).then_inc(a_att, 1)
                            wait(dve, a_att, a + 1)
                            nc.vector.tensor_tensor(row, row, att[:, :, :].rearrange("p h d -> p (h d)")[:, None, :],
                                                    ALU.add).then_inc(a_x1, 1)
                            wait(dve, a_x1, a + 1)
                            wait(dve, chain_n, STAT_STEPS * s)
                            dve.sem_inc(carried, 1)
                            nc.vector.bn_stats(stat[:, None, :], row).then_inc(a_stat, 1)

                        def second_stats(s, k, part):
                            count = [0 if part == 0 else 5]

                            def link(*instructions):
                                for instruction in instructions:
                                    count[0] += 1
                                    instruction.then_inc(chain_n, 1)
                                wait(dve, chain_n, STAT_STEPS * s + count[0])

                            source = stat[:, :] if values(k) else stats[:, s + AHEAD, :]
                            me, m2e, mo, m2o = (source[:, i:i + 1] for i in (1, 2, 4, 5))
                            m, diff, v, sq, less, y, half = (mv[:, i:i + 1] for i in range(7))
                            if part == 0:
                                if values(k):
                                    wait(dve, a_stat, s - 1)
                                wait(dve, rn_done, s)
                                link(nc.vector.tensor_scalar(m, me, mo, 0.5, ALU.add, ALU.mult),
                                     nc.vector.tensor_scalar(diff, me, mo, None, ALU.subtract),
                                     nc.vector.tensor_scalar(v, m2e, m2o, 1.0 / D, ALU.add, ALU.mult))
                                link(nc.vector.tensor_scalar(sq, diff, diff, 0.25, ALU.mult, ALU.mult))
                                link(nc.vector.tensor_scalar(v, v, sq, EPS, ALU.add, ALU.add))
                                return
                            link(nc.vector.tensor_scalar(y.bitcast(I32), v.bitcast(I32), -0.5, float(0x5F3759DF),
                                                         ALU.mult, ALU.add),
                                 nc.vector.tensor_scalar(less, v, -0.5, None, ALU.mult))
                            for _ in range(NEWTON):
                                link(nc.vector.tensor_scalar(half, y, y, less, ALU.mult, ALU.mult))
                                link(nc.vector.scalar_tensor_tensor(y, half, 1.5, y, ALU.add, ALU.mult))

                        def step(s, k):
                            hidden(s, 0)
                            if exps(k):
                                maximum(s)
                            split_lo(s, 0, k)
                            if routes(k - 1):
                                copy_weights(s - 1)
                            if exps(k):
                                less_maximum(s)
                            if k > 0:
                                add(s - 1)
                            hidden(s, 1)
                            if scores(k):
                                take_k(s)
                            split_lo(s, 1, k)
                            hidden(s, 2)
                            if values(k):
                                attend(s)
                            if routes(k):
                                second_stats(s, k, 0)
                            if routes(k):
                                second_stats(s, k, 1)
                            split_lo(s, 2, k)
                            hidden(s, 3)
                            if results(k):
                                result_row(s - AHEAD)
                            if routes(k):
                                norm(s, k)
                            split_lo(s, 3, k)
                            if exps(k):
                                denominators(s)
                            hidden(s, 4)
                            if routes(k):
                                route_lo(s)
                            split_lo(s, 4, k)
                            if routes(k):
                                pick(s)
                            if exps(k):
                                spread_values(s)
                            if turns(k):
                                norm_q(s)
                            hidden(s, 5)
                            split_lo(s, 5, k)
                            if routes(k):
                                weigh(s)

                        nc.vector.memset(vpair[:, :, :, :, :], 0.0).then_inc(a_vinit, 1)
                        dve.wait_ge(a_vinit, 1)
                        norm_q(-1)
                        over_steps(nc.vector, step)
                        add(NS - 1)
                        for f in range(NT - AHEAD, NT):
                            result_row(f)

                    @block.sync
                    def _(sp):
                        def context(s):
                            wait(sp, a_tqk, s + 1)
                            sp.dma_start(cnat[:, :], ctx_rows[bass.ds((s + NA + 1) * P, P), :]).then_inc(a_load, 16)

                        def step(s, k):
                            if turns(k):
                                context(s)
                            if exps(k):
                                wait(sp, a_v, s - 1)
                                src = ctx_rows[bass.ds((s + NA - 1) * P, P), :].rearrange("(b s) d -> s b d", b=2)
                                for half in range(2):
                                    sp.dma_start(cdup[64 * half:64 * half + 64, :, :], src).then_inc(a_cdup, 16)
                            if results(k):
                                store(s - AHEAD)

                        def store(f):
                            sp.wait_ge(fin_done, f + 1)
                            sp.dma_start(out_rows[bass.ds(f * P, P), :], xs[:, bass.ds(f, 1), :]).then_inc(stored, 16)

                        context(-1)
                        over_steps(nc.sync, step)
                        for f in range(NT - AHEAD, NT):
                            store(f)
                        sp.wait_ge(stored, 16 * NT)


_INS = ['x', 'ctx_2048', 'g_xattn', 'g_ffn', 'L0_ffn_gate_w', 'L0_ffn_w_gate', 'L0_ffn_w_up', 'L0_ffn_w_down']


def kernel(**inputs):
    import numpy as _np
    import concourse.bacc as _bacc
    from concourse import mybir as _mybir
    from concourse.bass_utils import run_bass_kernel_spmd as _run

    nc = _bacc.Bacc("TRN2", target_bir_lowering=False, num_devices=1)
    arrays, args = {}, []
    for name in _INS:
        a = _np.ascontiguousarray(inputs[name])
        arrays[f"in_{name}_dram"] = a
        args.append(nc.dram_tensor(f"in_{name}_dram", a.shape, _mybir.dt.from_np(a.dtype), kind="ExternalInput").ap())
    args.append(nc.dram_tensor("out_0_dram", arrays["in_x_dram"].shape, _mybir.dt.float32, kind="ExternalOutput").ap())
    build(nc, *args)
    r = _run(nc, [arrays], core_ids=[0])
    return r.results[0]["out_0_dram"]
```
